# Optimizing a Trainium2 kernel written in Bass

```python
import numpy as np
import jax
import jax.numpy as jnp

def _softmax(x, axis=-1):
    return jax.nn.softmax(x, axis=axis)

def _gelu(x):
    return jax.nn.gelu(x, approximate=True)

def _silu(x):
    return jax.nn.silu(x)

def _sigmoid(x):
    return jax.nn.sigmoid(x)

def _layernorm(x, axis=-1, eps=1e-05):
    m = jnp.mean(x, axis=axis, keepdims=True)
    v = jnp.var(x, axis=axis, keepdims=True)
    return (x - m) / jnp.sqrt(v + eps)

def _scatter_add(tgt, idx, src, axis=0):
    return tgt.at[idx].add(src)

def _segment_sum(src, seg, n):
    return jax.ops.segment_sum(src, seg, n)
kernel_name = 'mk_hybrid_d1_jaxref_r8_938b57'

def setup_inputs(seed: int=0):
    np.random.seed(seed)
    _w = jnp.asarray

    def _L0_attn_a_setup():
        import jax, jax.numpy as jnp
        import numpy as np
        NUM_HEADS = 16
        key = jax.random.key(seed)
        x = jax.random.normal(key, (4, 256, 128), dtype=jnp.float32)
        return {'x': x}
    _L0_attn_a_in = _L0_attn_a_setup()

    def _L0_attn_b_setup():
        import jax, jax.numpy as jnp
        import numpy as np
        BATCH, SEQ, HIDDEN = (8, 256, 128)
        WSIZE = 64
        NEG_INF = -1000000000.0
        key = jax.random.key(seed)
        k1, k2 = jax.random.split(key)
        repr_ = jax.random.normal(k1, (BATCH, SEQ, HIDDEN), dtype=jnp.float32)
        W = jax.random.normal(k2, (HIDDEN, HIDDEN), dtype=jnp.float32) * 0.02
        return {'repr': repr_, 'W': W}
    _L0_attn_b_in = _L0_attn_b_setup()

    def _L0_ffn_setup():
        import jax, jax.numpy as jnp
        import numpy as np
        D_MODEL = 128
        N_HEADS = 16
        HEAD_DIM = D_MODEL // N_HEADS
        KV_LATENT = 64
        N_EXPERTS = 4
        D_HIDDEN = 4 * D_MODEL
        B, T = (2, 128)

        def rmsnorm(x, w, eps=1e-06):
            return w * (x * jax.lax.rsqrt(jnp.mean(x * x, axis=-1, keepdims=True) + eps))

        def layernorm(x, g, b, eps=1e-05):
            mu = jnp.mean(x, axis=-1, keepdims=True)
            var = jnp.mean((x - mu) ** 2, axis=-1, keepdims=True)
            return (x - mu) * jax.lax.rsqrt(var + eps) * g + b

        def apply_rope(x):
            t, d = (x.shape[2], x.shape[3])
            half = d // 2
            pos = jnp.arange(t, dtype=x.dtype)[:, None]
            inv_freq = 1.0 / 10000.0 ** (jnp.arange(half, dtype=x.dtype) / half)
            ang = pos * inv_freq[None, :]
            sin, cos = (jnp.sin(ang), jnp.cos(ang))
            x1, x2 = (x[..., :half], x[..., half:])
            return jnp.concatenate([x1 * cos - x2 * sin, x1 * sin + x2 * cos], axis=-1)

        def mla_attention(x, Wq, Wdkv, Wuk, Wuv, Wo, ln_g, ln_b):
            b, t, _ = x.shape
            q = (x @ Wq.T).reshape(b, t, N_HEADS, HEAD_DIM).transpose(0, 2, 1, 3)
            latent = layernorm(x @ Wdkv.T, ln_g, ln_b)
            k = (latent @ Wuk.T).reshape(b, t, N_HEADS, HEAD_DIM).transpose(0, 2, 1, 3)
            v = (latent @ Wuv.T).reshape(b, t, N_HEADS, HEAD_DIM).transpose(0, 2, 1, 3)
            q = apply_rope(q)
            k = apply_rope(k)
            scores = jnp.einsum('bhqd,bhkd->bhqk', q, k) / np.sqrt(HEAD_DIM)
            causal = jnp.tril(jnp.ones((t, t), dtype=bool))
            scores = jnp.where(causal, scores, -jnp.inf)
            attn = jax.nn.softmax(scores, axis=-1)
            out = jnp.einsum('bhqk,bhkd->bhqd', attn, v).transpose(0, 2, 1, 3).reshape(b, t, D_MODEL)
            return out @ Wo.T

        def moe(x, gate_w, gate_b, W1, b1, W2, b2):
            logits = x @ gate_w.T + gate_b
            top = jnp.argmax(logits, axis=-1)
            onehot = jax.nn.one_hot(top, N_EXPERTS, dtype=x.dtype)
            h = jax.nn.relu(jnp.einsum('btd,ehd->bteh', x, W1) + b1)
            y = jnp.einsum('bteh,edh->bted', h, W2) + b2
            return jnp.einsum('bted,bte->btd', y, onehot)
        key = jax.random.key(seed)
        ks = jax.random.split(key, 16)
        s = lambda fan_in: 1.0 / np.sqrt(fan_in)
        return {'x': jax.random.normal(ks[0], (B, T, D_MODEL), jnp.float32), 'norm1_w': jnp.ones((D_MODEL,), jnp.float32), 'norm2_w': jnp.ones((D_MODEL,), jnp.float32), 'Wq': jax.random.normal(ks[1], (D_MODEL, D_MODEL), jnp.float32) * s(D_MODEL), 'Wdkv': jax.random.normal(ks[2], (KV_LATENT, D_MODEL), jnp.float32) * s(D_MODEL), 'Wuk': jax.random.normal(ks[3], (D_MODEL, KV_LATENT), jnp.float32) * s(KV_LATENT), 'Wuv': jax.random.normal(ks[4], (D_MODEL, KV_LATENT), jnp.float32) * s(KV_LATENT), 'Wo': jax.random.normal(ks[5], (D_MODEL, D_MODEL), jnp.float32) * s(D_MODEL), 'ln_g': jnp.ones((KV_LATENT,), jnp.float32), 'ln_b': jnp.zeros((KV_LATENT,), jnp.float32), 'gate_w': jax.random.normal(ks[6], (N_EXPERTS, D_MODEL), jnp.float32) * s(D_MODEL), 'gate_b': jnp.zeros((N_EXPERTS,), jnp.float32), 'W1': jax.random.normal(ks[7], (N_EXPERTS, D_HIDDEN, D_MODEL), jnp.float32) * s(D_MODEL), 'b1': jnp.zeros((N_EXPERTS, D_HIDDEN), jnp.float32), 'W2': jax.random.normal(ks[8], (N_EXPERTS, D_MODEL, D_HIDDEN), jnp.float32) * s(D_HIDDEN), 'b2': jnp.zeros((N_EXPERTS, D_MODEL), jnp.float32)}
    _L0_ffn_in = _L0_ffn_setup()
    _d = {'L0_attn_a_x': _L0_attn_a_in['x'], 'L0_attn_b_W': _L0_attn_b_in['W'], 'L0_ffn_norm1_w': _L0_ffn_in['norm1_w'], 'L0_ffn_norm2_w': _L0_ffn_in['norm2_w'], 'L0_ffn_Wq': _L0_ffn_in['Wq'], 'L0_ffn_Wdkv': _L0_ffn_in['Wdkv'], 'L0_ffn_Wuk': _L0_ffn_in['Wuk'], 'L0_ffn_Wuv': _L0_ffn_in['Wuv'], 'L0_ffn_Wo': _L0_ffn_in['Wo'], 'L0_ffn_ln_g': _L0_ffn_in['ln_g'], 'L0_ffn_ln_b': _L0_ffn_in['ln_b'], 'L0_ffn_gate_w': _L0_ffn_in['gate_w'], 'L0_ffn_gate_b': _L0_ffn_in['gate_b'], 'L0_ffn_W1': _L0_ffn_in['W1'], 'L0_ffn_b1': _L0_ffn_in['b1'], 'L0_ffn_W2': _L0_ffn_in['W2'], 'L0_ffn_b2': _L0_ffn_in['b2']}
    _x0 = _d['L0_attn_a_x']
    _d['L0_attn_a_x'] = jax.random.normal(jax.random.fold_in(jax.random.key(seed), 1), (32, 256, 128), dtype=_x0.dtype)
    del _x0
    return _d

def reference(L0_attn_a_x, L0_attn_b_W, L0_ffn_norm1_w, L0_ffn_norm2_w, L0_ffn_Wq, L0_ffn_Wdkv, L0_ffn_Wuk, L0_ffn_Wuv, L0_ffn_Wo, L0_ffn_ln_g, L0_ffn_ln_b, L0_ffn_gate_w, L0_ffn_gate_b, L0_ffn_W1, L0_ffn_b1, L0_ffn_W2, L0_ffn_b2):

    def _L0_attn_a_ref(x):
        import jax, jax.numpy as jnp
        import numpy as np
        NUM_HEADS = 16
        B, T, D = x.shape
        H = NUM_HEADS
        hd = D // H
        xh = x.reshape(B, T, H, hd)
        x_centered = xh - jnp.mean(xh, axis=1, keepdims=True)
        corr = jnp.einsum('bthd,bThd->bhtT', x_centered, x_centered)
        corr = jax.nn.softmax(corr, axis=-1)
        out = jnp.einsum('bhtT,bThd->bthd', corr, xh)
        return out.reshape(B, T, D)

    def _L0_attn_b_ref(repr, W):
        import jax, jax.numpy as jnp
        import numpy as np
        BATCH, SEQ, HIDDEN = (8, 256, 128)
        WSIZE = 64
        NEG_INF = -1000000000.0
        b, s, d = repr.shape
        idx = jnp.arange(s)
        mask = jnp.abs(idx[:, None] - idx[None, :]) > WSIZE
        scores = jnp.einsum('bqd,de,bke->bqk', repr, W, repr)
        scores = jnp.where(mask[None, :, :], NEG_INF, scores)
        probs = jax.nn.softmax(scores, axis=-1)
        ra = jnp.einsum('bqk,bkd->bqd', probs, repr)
        return repr + jax.nn.relu(ra)

    def _L0_ffn_ref(x, norm1_w, norm2_w, Wq, Wdkv, Wuk, Wuv, Wo, ln_g, ln_b, gate_w, gate_b, W1, b1, W2, b2):
        import jax, jax.numpy as jnp
        import numpy as np
        D_MODEL = 128
        N_HEADS = 16
        HEAD_DIM = D_MODEL // N_HEADS
        KV_LATENT = 64
        N_EXPERTS = 4
        D_HIDDEN = 4 * D_MODEL
        B, T = (2, 128)

        def rmsnorm(x, w, eps=1e-06):
            return w * (x * jax.lax.rsqrt(jnp.mean(x * x, axis=-1, keepdims=True) + eps))

        def layernorm(x, g, b, eps=1e-05):
            mu = jnp.mean(x, axis=-1, keepdims=True)
            var = jnp.mean((x - mu) ** 2, axis=-1, keepdims=True)
            return (x - mu) * jax.lax.rsqrt(var + eps) * g + b

        def apply_rope(x):
            t, d = (x.shape[2], x.shape[3])
            half = d // 2
            pos = jnp.arange(t, dtype=x.dtype)[:, None]
            inv_freq = 1.0 / 10000.0 ** (jnp.arange(half, dtype=x.dtype) / half)
            ang = pos * inv_freq[None, :]
            sin, cos = (jnp.sin(ang), jnp.cos(ang))
            x1, x2 = (x[..., :half], x[..., half:])
            return jnp.concatenate([x1 * cos - x2 * sin, x1 * sin + x2 * cos], axis=-1)

        def mla_attention(x, Wq, Wdkv, Wuk, Wuv, Wo, ln_g, ln_b):
            b, t, _ = x.shape
            q = (x @ Wq.T).reshape(b, t, N_HEADS, HEAD_DIM).transpose(0, 2, 1, 3)
            latent = layernorm(x @ Wdkv.T, ln_g, ln_b)
            k = (latent @ Wuk.T).reshape(b, t, N_HEADS, HEAD_DIM).transpose(0, 2, 1, 3)
            v = (latent @ Wuv.T).reshape(b, t, N_HEADS, HEAD_DIM).transpose(0, 2, 1, 3)
            q = apply_rope(q)
            k = apply_rope(k)
            scores = jnp.einsum('bhqd,bhkd->bhqk', q, k) / np.sqrt(HEAD_DIM)
            causal = jnp.tril(jnp.ones((t, t), dtype=bool))
            scores = jnp.where(causal, scores, -jnp.inf)
            attn = jax.nn.softmax(scores, axis=-1)
            out = jnp.einsum('bhqk,bhkd->bhqd', attn, v).transpose(0, 2, 1, 3).reshape(b, t, D_MODEL)
            return out @ Wo.T

        def moe(x, gate_w, gate_b, W1, b1, W2, b2):
            logits = x @ gate_w.T + gate_b
            top = jnp.argmax(logits, axis=-1)
            onehot = jax.nn.one_hot(top, N_EXPERTS, dtype=x.dtype)
            h = jax.nn.relu(jnp.einsum('btd,ehd->bteh', x, W1) + b1)
            y = jnp.einsum('bteh,edh->bted', h, W2) + b2
            return jnp.einsum('bted,bte->btd', y, onehot)
        x = x + mla_attention(rmsnorm(x, norm1_w), Wq, Wdkv, Wuk, Wuv, Wo, ln_g, ln_b)
        x = x + moe(rmsnorm(x, norm2_w), gate_w, gate_b, W1, b1, W2, b2)
        return x
    x = L0_attn_a_x
    x = x + _L0_attn_a_ref(_layernorm(x, axis=-1))
    x = x + _L0_ffn_ref(_layernorm(x, axis=-1), L0_ffn_norm1_w, L0_ffn_norm2_w, L0_ffn_Wq, L0_ffn_Wdkv, L0_ffn_Wuk, L0_ffn_Wuv, L0_ffn_Wo, L0_ffn_ln_g, L0_ffn_ln_b, L0_ffn_gate_w, L0_ffn_gate_b, L0_ffn_W1, L0_ffn_b1, L0_ffn_W2, L0_ffn_b2)
    x = x + _L0_attn_b_ref(_layernorm(x, axis=-1), L0_attn_b_W)
    x = x + _L0_ffn_ref(_layernorm(x, axis=-1), L0_ffn_norm1_w, L0_ffn_norm2_w, L0_ffn_Wq, L0_ffn_Wdkv, L0_ffn_Wuk, L0_ffn_Wuv, L0_ffn_Wo, L0_ffn_ln_g, L0_ffn_ln_b, L0_ffn_gate_w, L0_ffn_gate_b, L0_ffn_W1, L0_ffn_b1, L0_ffn_W2, L0_ffn_b2)
    return x

_drawn_inputs = setup_inputs


def setup_inputs(seed=0):
    import zlib

    import numpy as np

    out = dict(_drawn_inputs(seed))
    spreads = {'L0_ffn_norm1_w': (1.0, 0.2),
     'L0_ffn_norm2_w': (1.0, 0.2),
     'L0_ffn_ln_g': (1.0, 0.2),
     'L0_ffn_ln_b': (0.0, 0.1),
     'L0_ffn_gate_b': (0.0, 0.1),
     'L0_ffn_b1': (0.0, 0.1),
     'L0_ffn_b2': (0.0, 0.1)}
    factors = {}
    for name, (base, spread) in spreads.items():
        noise = np.random.default_rng([zlib.crc32(name.encode()), seed]).standard_normal(out[name].shape)
        drawn = base * np.exp(spread * noise) if base else spread * noise
        out[name] = jnp.asarray(drawn.astype(out[name].dtype))
    for name, factor in factors.items():
        out[name] = (out[name] * factor).astype(out[name].dtype)
    return out
```

```python
from contextlib import ExitStack

import concourse.bass as bass
from concourse import mybir

F32 = mybir.dt.float32
BF16 = mybir.dt.bfloat16
ALU = mybir.AluOpType
ACT = mybir.ActivationFunctionType
AX = mybir.AxisListType.X

B, T, D = 32, 256, 128
P = 128
TC = T // P
H, HD = 16, 8
G, V = 4, 4
QUAD = 32
LAT = 64
E, HID = 4, 512
J = HID // P
PIECES = 3 * E
BAND = 64
LN_EPS, RMS_EPS = 1e-5, 1e-6
BIG = 1e30
K2_ROWS = 2 * QUAD + V

CST, CST_COLS = {}, 0
for _name, _n in (("ident", P), ("qmask0", V * P), ("qmask1", 2 * T), ("kmask0", 2 * T), ("kmask1", V * P),
                  ("band", TC * T), ("cos_q", T), ("sin_q", T), ("cos_k", T), ("sin_k", T),
                  ("headmask", V), ("shiftsel", V), ("priority", E)):
    CST[_name] = (CST_COLS, CST_COLS + _n)
    CST_COLS += _n
QM0, QM1, KM0, KM1 = range(4)

PLACE = {
    "full": {"pro0": [0, 1], "pro1": [2, 3], "core": {}},
    "band": {"pro0": [0, 1], "pro1": [2, 3], "core": {}},
    "causal": {"pro0": [4, 5], "pro1": [6, 7], "pro2": [8, 9, 10], "core": {}, "post": [11]},
}


class Core:

    def __init__(self, kind, sem):
        self.kind, self.causal = kind, kind == "causal"
        if self.causal:
            self.q_units = [(0, 0, V, P), (1, 0, 2, T), (1, 2, 2, T)]
            self.k_units = [(0, 0, 2, 0), (0, 2, 2, 0), (1, 0, V, P)]
        else:
            self.q_units = [(c, v, 2, T) for c in range(TC) for v in (0, 2)]
            self.k_units = [(c, v, 2, 0) for c in range(TC) for v in (0, 2)]
        self.nq, self.nk = len(self.q_units), len(self.k_units)
        self.high, self.mid, self.low = (sem(f"{kind}_{n}_part") for n in ("high", "mid", "low"))
        self.stack1 = sem(f"{kind}_stack1_loaded")
        self.stack2 = sem(f"{kind}_stack2_loaded")
        self.k1 = sem(f"{kind}_k1_masked")
        self.k2 = sem(f"{kind}_k2_masked")
        self.values = sem(f"{kind}_values_ready")
        self.scores_q = sem(f"{kind}_scores_q")
        self.maxed = sem(f"{kind}_maxed")
        self.max_t = sem(f"{kind}_max_transposed")
        self.shift = sem(f"{kind}_shift_ready")
        self.scores_k = sem(f"{kind}_scores_k")
        self.probs = sem(f"{kind}_probs_ready")
        self.weighted = sem(f"{kind}_weighted")
        self.weighted_sb = sem(f"{kind}_weighted_sb")
        self.out_t = sem(f"{kind}_out_transposed")
        self.recip = sem(f"{kind}_denominators")
        self.normed = sem(f"{kind}_normed")


class Norm:

    def __init__(self, kind, sem):
        self.chain = sem(f"{kind}_dve_chain")
        self.var, self.rstd = sem(f"{kind}_var"), sem(f"{kind}_rstd")
        self.done = sem(f"{kind}_normalised")
        self.t, self.t_sb = sem(f"{kind}_norm_t"), sem(f"{kind}_norm_t_sb")


CHAIN_FULL, CHAIN_CAUSAL, CHAIN_BAND = 6, 22, 7


def build(nc, x, wb, wq, wqr, wdkv, wuk, wukr, wuv, wo, gate, w1, w2, b1, b2, gate_b, cols, cst, out):
    with ExitStack() as ctx:
        def sb(name, shape, dt=F32):
            return ctx.enter_context(nc.sbuf_tensor(name, shape, dt))

        def sem(name):
            return ctx.enter_context(nc.semaphore(name))

        w_b = sb("w_b", [P, D])
        w_q, w_qr = sb("w_q", [P, D]), sb("w_qr", [P, D])
        w_dkv = sb("w_dkv", [P, LAT])
        w_uk, w_ukr, w_uv = sb("w_uk", [LAT, D]), sb("w_ukr", [LAT, D]), sb("w_uv", [LAT, D])
        w_o = sb("w_o", [P, D])
        w_gate = sb("w_gate", [P, E])
        w_1 = sb("w_1", [P, E, HID])
        w_2 = sb("w_2", [P, E, J, D])
        b_1 = sb("b_1", [P, E * J])
        b_2 = sb("b_2", [P, E, D])
        b_gate = sb("b_gate", [P, E])
        col = sb("col", [P, 4])
        c_sb = sb("c_sb", [P, CST_COLS])
        ident_b = sb("ident_b", [P, P], BF16)
        masks_b = sb("masks_b", [P, 4, 512], BF16)
        minus_half = sb("minus_half", [P, TC])

        def const(name):
            a, b = CST[name]
            return c_sb[:, a:b]

        ident = const("ident")

        x_all = sb("x_all", [P, B * T])
        x_in = sb("x_in", [P, T])
        x_mid = sb("x_mid", [P, T])
        z = sb("z", [P, TC, D])
        zr = sb("zr", [P, TC, D])
        z_t = sb("z_t", [P, T])
        stats = sb("stats", [P, TC, 6])
        mv = sb("mv", [P, TC, 2])
        var_eps, rstd = sb("var_eps", [P, TC]), sb("rstd", [P, TC])
        sqr = sb("sqr", [P, TC])
        ms, rrms = sb("ms", [P, TC]), sb("rrms", [P, TC])
        lat_n = sb("lat_n", [P, TC, P])
        lat_t = sb("lat_t", [LAT, T])
        rope_a, rope_b = sb("rope_a", [P, T]), sb("rope_b", [P, T])
        mean = sb("mean", [P, 2])
        spacer = sb("spacer", [P, 1])
        qk = sb("qk", [P, 2, T])
        rest = sb("rest", [P, 2, T])
        high, mid, low = (sb(f"{n}_part", [P, 2, T], BF16) for n in ("high", "mid", "low"))
        q1 = sb("q1", [P, G, T], BF16)
        k1_raw = sb("k1_raw", [P, G, T], BF16)
        k1 = sb("k1", [P, G, V, T], BF16)
        q2 = sb("q2", [P, G, T], BF16)
        k2_raw = sb("k2_raw", [2 * QUAD, G, T], BF16)
        k2 = sb("k2", [P, G, V, T], BF16)
        maxima = sb("maxima", [P, G, TC, V], BF16)
        probs = sb("probs", [P, 2, TC, V, T])
        values = sb("values", [P, TC, H, QUAD])
        wt_sb = sb("wt_sb", [P, 2, T])
        rsum = sb("rsum", [P, G, TC, V])
        att = sb("att", [P, TC, H, HD])
        att_t = sb("att_t", [P, T])
        y1 = sb("y1", [P, TC, D])
        sq = sb("sq", [P, TC, D])
        xm_t = sb("xm_t", [P, T])
        logits = sb("logits", [P, TC, E])
        lmax, rmax = sb("lmax", [P, TC]), sb("rmax", [P, TC])
        ranked = sb("ranked", [P, TC, E])
        onehot = sb("onehot", [P, TC, E])
        hidden = sb("hidden", [P, 2, J, T])
        y_b = sb("y_b", [P, TC, D])
        acc = sb("acc", [P, T])
        t_t = sb("t_t", [P, T])
        s_band = sb("s_band", [P, TC, T])
        p_band, pt_band = sb("p_band", [P, TC, T]), sb("pt_band", [P, TC, T])
        bmax, nmax = sb("bmax", [P, TC]), sb("nmax", [P, TC])
        sum_band, r_band = sb("sum_band", [P, TC]), sb("r_band", [P, TC])
        xz, ra = sb("xz", [P, T]), sb("ra", [P, TC, D])

        bank = [ctx.enter_context(nc.psum_tensor(f"bank{i}", [P, 512], F32)) for i in range(8)]
        SQ, SK, WT, TR, EX = bank[0:2], bank[2:4], bank[4], bank[5], bank[6:8]
        tr_max = TR[:, 256:384].bitcast(BF16)

        loaded, consts_ready, zeroed, ones_set = sem("weights_loaded"), sem("consts_ready"), sem("zeroed"), sem("ones_set")
        x_loaded, x_moved = sem("x_loaded"), sem("x_moved")
        full, causal = Core("full", sem), Core("causal", sem)
        f_n, c_n, b_n = Norm("full", sem), Norm("causal", sem), Norm("band", sem)
        x_mid_a, x_mid_b = sem("x_mid_pass_a"), sem("x_mid_pass_b")
        c_ms, c_rrms = sem("z_mean_square"), sem("z_inverse_rms")
        lat_ps, lat_var, lat_rstd = sem("latent_psum"), sem("latent_var"), sem("latent_rstd")
        lat_done, lat_tps, lat_tsb = sem("latent_normalised"), sem("latent_t_psum"), sem("latent_t_sb")
        q_ps, k_ps, v_ps = sem("q_psum"), sem("k_psum"), sem("v_psum")
        att_tps, att_tsb, y_ps = sem("att_t_psum"), sem("att_t_sb"), sem("att_projected")
        y_ms, y_rrms = sem("y_mean_square"), sem("y_inverse_rms")
        xm_done, xm_tps, xm_tsb, logit_ps = sem("xm_ready"), sem("xm_t_psum"), sem("xm_t_sb"), sem("logits_psum")
        t_ps, t_sb, s_ps, bmax_done = sem("band_t_psum"), sem("band_t_sb"), sem("band_scores"), sem("band_max")
        p_done, pt_ps, pt_sb, ra_ps = sem("band_probs"), sem("band_pt_psum"), sem("band_pt_sb"), sem("band_weighted")
        up, relu, down = sem("expert_up"), sem("expert_relu"), sem("expert_down")
        biased, combined = sem("expert_biased"), sem("expert_combined")
        kept, stored = sem("acc_kept"), sem("stored")

        x_d = x.rearrange("b (c p) d -> b p c d", p=P)
        out_d = out.rearrange("b (c p) d -> b p c d", p=P)

        LOADS = [(w_b[:], wb), (w_q[:], wq), (w_qr[:], wqr), (w_dkv[:], wdkv), (w_uk[:], wuk), (w_ukr[:], wukr),
                 (w_uv[:], wuv), (w_o[:], wo), (w_gate[:], gate), (w_1[:], w1), (w_2[:], w2), (b_1[:], b1),
                 (b_2[:], b2), (b_gate[:], gate_b), (col[:], cols), (c_sb[:], cst)]
        ALL_LOADED = 16 * len(LOADS)

        def run(engine, first_a, first_b, second, experts, keep):
            for base, first in ((0, first_a), (B, first_b)):
                first(0, None)
                second(base, 0, None)
                with engine.Fori(1, B, 1) as i:
                    first(i, base - 1 + i)
                    second(base + i, i, base - 1 + i)
                for k in range(PIECES):
                    experts(k, base + B - 1)
                keep(base, B - 1)

        def pieces(experts, m, kind, slot):
            if m is not None:
                for k in PLACE[kind].get(slot, ()):
                    experts(k, m)

        block = ctx.enter_context(nc.Block())

        @block.sync
        def _(sp):
            for dst, src in LOADS:
                sp.dma_start(dst, src).then_inc(loaded, 16)

            def stack(core, n):
                kk = 1 if core.causal else 0
                sp.wait_ge(core.high, n + 1)
                for dst, quad, which in ((q1, 0, 0), (q1, 2, 0), (k1_raw, 0, kk), (k1_raw, 1, kk)):
                    sp.dma_start(dst[quad * QUAD:(quad + 1) * QUAD, :, :].rearrange("r g t -> r (g t)"), high[:, which, :]).then_inc(core.stack1, 16)
                sp.wait_ge(core.mid, n + 1)
                for dst, quad, which in ((q1, 1, 0), (q1, 3, 0), (k1_raw, 2, kk), (k1_raw, 3, kk)):
                    sp.dma_start(dst[quad * QUAD:(quad + 1) * QUAD, :, :].rearrange("r g t -> r (g t)"), mid[:, which, :]).then_inc(core.stack1, 16)
                for dst, quad, which in ((q2, 1, 0), (k2_raw, 0, kk)):
                    sp.dma_start(dst[quad * QUAD:(quad + 1) * QUAD, :, :].rearrange("r g t -> r (g t)"), high[:, which, :]).then_inc(core.stack2, 16)
                sp.wait_ge(core.low, n + 1)
                for dst, quad, which in ((q2, 0, 0), (k2_raw, 1, kk)):
                    sp.dma_start(dst[quad * QUAD:(quad + 1) * QUAD, :, :].rearrange("r g t -> r (g t)"), low[:, which, :]).then_inc(core.stack2, 16)

            def full_stage(b, m):
                if m is not None:
                    sp.wait_ge(x_mid_a, b)
                sp.dma_start(x_in[:].rearrange("p (c d) -> p c d", c=TC), x_d[bass.ds(b, 1), :, :, :].rearrange("o p c d -> (o p) c d")).then_inc(x_loaded, 16)
                stack(full, b)

            def band_stage(b, m):
                if m is None:
                    sp.wait_ge(x_mid_a, B)
                    sp.wait_ge(kept, 16 * B)
                else:
                    sp.wait_ge(x_mid_b, b)
                sp.dma_start(x_in[:], x_all[:, bass.ds(b * T, T)]).then_inc(x_moved, 16)

            def store(base, b):
                sp.wait_ge(combined, (base + b) * E + E)
                if base:
                    sp.dma_start(out_d[bass.ds(b, 1), :, :, :].rearrange("o p c d -> (o p) c d"), acc[:].rearrange("p (c d) -> p c d", c=TC)).then_inc(stored, 16)
                else:
                    sp.dma_start(x_all[:, bass.ds(b * T, T)], acc[:]).then_inc(kept, 16)

            for base, first in ((0, full_stage), (B, band_stage)):
                first(0, None)
                stack(causal, base)
                with sp.Fori(1, B, 1) as i:
                    first(i, i)
                    stack(causal, base + i)
                    store(base, i - 1)
                store(base, B - 1)
            sp.wait_ge(stored, 16 * B)

        @block.gpsimd
        def _(pool):
            nc.gpsimd.memset(values[:], 0.0).then_inc(zeroed, 1)
            nc.gpsimd.memset(lat_n[:], 0.0).then_inc(zeroed, 1)
            nc.gpsimd.memset(minus_half[:], -0.5).then_inc(zeroed, 1)
            pool.wait_ge(zeroed, 3)
            nc.gpsimd.memset(values[:, :, :, HD:HD + 1], 1.0).then_inc(ones_set, 1)
            pool.wait_ge(ones_set, 1)

            def inverse_root(dst, src, ready, done, n):
                pool.wait_ge(ready, n + 1)
                nc.gpsimd.tensor_tensor(dst[:], src[:], minus_half[:], ALU.pow).then_inc(done, 1)

            def full_stage(b, m):
                inverse_root(rstd, var_eps, f_n.var, f_n.rstd, b)

            def band_stage(b, m):
                inverse_root(rstd, var_eps, b_n.var, b_n.rstd, b)

            def causal_stage(n):
                inverse_root(rstd, var_eps, c_n.var, c_n.rstd, n)
                inverse_root(rrms, ms, c_ms, c_rrms, n)
                inverse_root(rstd, var_eps, lat_var, lat_rstd, n)
                inverse_root(rrms, ms, y_ms, y_rrms, n)

            for base, first in ((0, full_stage), (B, band_stage)):
                first(0, None)
                causal_stage(base)
                with pool.Fori(1, B, 1) as i:
                    first(i, i)
                    causal_stage(base + i)

        @block.scalar
        def _(act):
            act.wait_ge(loaded, ALL_LOADED)
            act.wait_ge(ones_set, 1)

            def experts(k, m):
                e, u = divmod(k, 3)
                if u == 2:
                    return
                act.wait_ge(up, m * (2 * E) + 2 * e + u + 1)
                if e >= 2 and u == 0:
                    act.wait_ge(down, m * E + e - 1)
                for i in range(2):
                    j = 2 * u + i
                    last = nc.scalar.activation(hidden[:, e % 2, j, :], EX[k % 2][:, i * T:(i + 1) * T], ACT.Relu,
                                                bias=b_1[:, e * J + j:e * J + j + 1])
                last.then_inc(relu, 1)

            def mask_k2(core, n):
                act.wait_ge(core.stack2, n * 64 + 64)
                for v in range(V):
                    nc.scalar.activation(k2[0:2 * QUAD, :, v, :], k2_raw[:], ACT.Copy,
                                         scale=const("headmask")[0:2 * QUAD, v:v + 1]).then_inc(core.k2, 1)

            def copy_weighted(core, n, g):
                act.wait_ge(core.weighted, n * G + g + 1)
                nc.scalar.copy(wt_sb[:, g % 2, :], WT[:, 0:T]).then_inc(core.weighted_sb, 1)

            def attend(core, n, m):
                for g in range(G):
                    for u, (kc, v0, nv, q0) in enumerate(core.k_units):
                        idx = g * core.nk + u
                        act.wait_ge(core.scores_k, n * (G * core.nk) + idx + 1)
                        if u == 0 and g >= 2:
                            act.wait_ge(core.weighted, n * G + g - 1)
                        w = T - q0
                        nc.scalar.activation(probs[:, g % 2, kc, v0:v0 + nv, q0:T],
                                             SK[idx % 2][:, 0:nv * w].rearrange("p (v q) -> p v q", q=w),
                                             ACT.Exp).then_inc(core.probs, 1)
                    if g >= 1:
                        copy_weighted(core, n, g - 1)
                copy_weighted(core, n, G - 1)

            def full_stage(b, m):
                act.wait_ge(f_n.done, b + 1)
                for c in range(TC):
                    last = nc.scalar.copy(values[:, c, :, 0:HD].rearrange("p (g v) e -> p g v e", g=G),
                                          z[:, c, :].rearrange("p (v e g) -> p g v e", v=V, e=HD))
                last.then_inc(full.values, 1)
                pieces(experts, m, "full", "pro0")
                pieces(experts, m, "full", "pro1")
                mask_k2(full, b)
                attend(full, b, m)

            def band_stage(b, m):
                pieces(experts, m, "band", "pro0")
                act.wait_ge(t_ps, b + 1)
                nc.scalar.copy(t_t[:], SQ[1][:, 0:T]).then_inc(t_sb, 1)
                pieces(experts, m, "band", "pro1")
                act.wait_ge(bmax_done, b + 1)
                for c in range(TC):
                    last = nc.scalar.activation(p_band[:, c, :], s_band[:, c, :], ACT.Exp, bias=nmax[:, c:c + 1],
                                                accum_out=sum_band[:, c:c + 1])
                last.then_inc(p_done, 1)
                act.wait_ge(pt_ps, b + 1)
                nc.scalar.copy(pt_band[:].rearrange("p c q -> p (c q)"), SK[1][:, 0:TC * T]).then_inc(pt_sb, 1)

            def causal_stage(n, b, m):
                pieces(experts, m, "causal", "pro0")
                pieces(experts, m, "causal", "pro1")
                act.wait_ge(v_ps, n + 1)
                for c in range(TC):
                    last = nc.scalar.copy(values[:, c, :, 0:HD], SK[0][:, c * D:(c + 1) * D].rearrange("p (h e) -> p h e", e=HD))
                last.then_inc(causal.values, 1)
                pieces(experts, m, "causal", "pro2")
                mask_k2(causal, n)
                attend(causal, n, m)
                act.wait_ge(att_tps, n + 1)
                nc.scalar.copy(att_t[:], SQ[0][:, 0:T]).then_inc(att_tsb, 1)
                pieces(experts, m, "causal", "post")

            run(act, full_stage, band_stage, causal_stage, experts, lambda base, b: None)

        @block.vector
        def _(dve):
            dve.wait_ge(loaded, ALL_LOADED)
            dve.wait_ge(ones_set, 1)
            nc.vector.tensor_copy(ident_b[:], ident)
            for i, name in enumerate(("qmask0", "qmask1", "kmask0", "kmask1")):
                nc.vector.tensor_copy(masks_b[:, i, :], const(name))
            nc.vector.memset(k2[2 * QUAD:K2_ROWS, :, :, :], 1.0).then_inc(consts_ready, 1)
            dve.wait_ge(consts_ready, 1)
            for v in range(V):
                last = nc.vector.tensor_scalar(k2[2 * QUAD:K2_ROWS, :, v, :], k2[2 * QUAD:K2_ROWS, :, v, :],
                                               const("shiftsel")[2 * QUAD:K2_ROWS, v:v + 1], None, ALU.mult)
            last.then_inc(consts_ready, 1)

            step = [0]

            def chain_of(norm, per, n):
                step[0] = 0

                def link(ins):
                    step[0] += 1
                    assert step[0] <= per, (norm, per)
                    ins.then_inc(norm.chain, 1)
                    dve.wait_ge(norm.chain, n * per + step[0])
                return link

            def experts(k, m):
                e, u = divmod(k, 3)
                if u != 2:
                    return
                dve.wait_ge(down, m * E + e + 1)
                nc.vector.tensor_tensor(y_b[:], EX[k % 2][:, 0:T].rearrange("p (c d) -> p c d", c=TC),
                                        b_2[:, e:e + 1, :].to_broadcast([P, TC, D]), ALU.add).then_inc(biased, 1)
                dve.wait_ge(biased, m * E + e + 1)
                if e:
                    dve.wait_ge(combined, m * E + e)
                for c in range(TC):
                    last = nc.vector.scalar_tensor_tensor(acc[:, c * D:(c + 1) * D], y_b[:, c, :], onehot[:, c, e:e + 1],
                                                          acc[:, c * D:(c + 1) * D], ALU.mult, ALU.add)
                last.then_inc(combined, 1)

            def moments(link, src, width):
                for c in range(TC):
                    last = nc.vector.bn_stats(stats[:, c, :], src[:, c * width:(c + 1) * width])
                link(last)
                nc.vector.memset(spacer[:], 0.0)
                for c in range(TC):
                    last = nc.vector.bn_aggr(mv[:, c, :], stats[:, c, :])
                link(last)

            def inverse_std(ready, done, n):
                nc.vector.tensor_scalar(var_eps[:], mv[:, :, 1], LN_EPS, None, ALU.add).then_inc(ready, 1)
                dve.wait_ge(done, n + 1)

            def normalise(dst, src, width):
                for c in range(TC):
                    last = nc.vector.tensor_scalar(dst[:, c, :], src[:, c * width:(c + 1) * width], mv[:, c, 0:1],
                                                   rstd[:, c:c + 1], ALU.subtract, ALU.mult)
                return last

            def split(core, link, n, w):
                nc.vector.tensor_copy(high[:, 0:w, :], qk[:, 0:w, :]).then_inc(core.high, 1)
                dve.wait_ge(core.high, n + 1)
                link(nc.vector.tensor_tensor(rest[:, 0:w, :], qk[:, 0:w, :], high[:, 0:w, :], ALU.subtract))
                nc.vector.tensor_copy(mid[:, 0:w, :], rest[:, 0:w, :]).then_inc(core.mid, 1)
                dve.wait_ge(core.mid, n + 1)
                nc.vector.tensor_tensor(low[:, 0:w, :], rest[:, 0:w, :], mid[:, 0:w, :], ALU.subtract).then_inc(core.low, 1)

            def mask_k1(core, n):
                dve.wait_ge(core.stack1, n * 128 + 128)
                for v in range(V):
                    nc.vector.tensor_scalar(k1[:, :, v, :], k1_raw[:], const("headmask")[:, v:v + 1], None,
                                            ALU.mult).then_inc(core.k1, 1)

            def attend(core, n, m):
                def row_max(g, u):
                    c, v0, nv, keys = core.q_units[u]
                    idx = g * core.nq + u
                    dve.wait_ge(core.scores_q, n * (G * core.nq) + idx + 1)
                    nc.vector.reduce_max(maxima[:, g, c, v0:v0 + nv],
                                         SQ[idx % 2][:, 0:nv * keys].rearrange("p (v k) -> p v k", k=keys),
                                         AX).then_inc(core.maxed, 1)

                def take_shift(g):
                    dve.wait_ge(core.max_t, n * G + g + 1)
                    nc.vector.tensor_copy(q2[2 * QUAD:K2_ROWS, g, :], tr_max[2 * QUAD:K2_ROWS, :]).then_inc(core.shift, 1)

                def divide(g):
                    dve.wait_ge(core.out_t, n * G + g + 1)
                    o = TR[:, 0:T].rearrange("p (c v r) -> p c v r", c=TC, r=QUAD)
                    nc.vector.reciprocal(rsum[:, g, :, :], o[:, :, :, HD]).then_inc(core.recip, 1)
                    dve.wait_ge(core.recip, n * G + g + 1)
                    nc.vector.tensor_tensor(att[:, :, g * V:(g + 1) * V, :], o[:, :, :, 0:HD],
                                            rsum[:, g, :, :].unsqueeze(3).to_broadcast([P, TC, V, HD]), ALU.mult).then_inc(core.normed, 1)

                for u in range(core.nq):
                    row_max(0, u)
                for g in range(G):
                    more = g + 1 < G
                    if more:
                        row_max(g + 1, 0)
                    take_shift(g)
                    if more:
                        for u in range(1, core.nq):
                            row_max(g + 1, u)
                    if g:
                        divide(g - 1)
                divide(G - 1)
                dve.wait_ge(core.normed, n * G + G)

            def full_stage(b, m):
                link = chain_of(f_n, CHAIN_FULL, b)
                dve.wait_ge(x_loaded, b * 16 + 16)
                moments(link, x_in, D)
                inverse_std(f_n.var, f_n.rstd, b)
                for c in range(TC):
                    last = nc.vector.tensor_scalar(z[:, c, :].rearrange("p (r g) -> p g r", g=G),
                                                   x_in[:, c * D:(c + 1) * D].rearrange("p (g r) -> p g r", g=G),
                                                   mv[:, c, 0:1], rstd[:, c:c + 1], ALU.subtract, ALU.mult)
                last.then_inc(f_n.done, 1)
                pieces(experts, m, "full", "pro0")
                dve.wait_ge(f_n.t, b + 1)
                link(nc.vector.reduce_sum(mean[:, 0:1], SQ[0][:, 0:T], AX))
                link(nc.vector.tensor_scalar(mean[:, 1:2], mean[:, 0:1], 1.0 / T, None, ALU.mult))
                link(nc.vector.tensor_scalar(qk[:, 0, :], SQ[0][:, 0:T], mean[:, 1:2], None, ALU.subtract))
                split(full, link, b, 1)
                pieces(experts, m, "full", "pro1")
                mask_k1(full, b)
                attend(full, b, m)
                nc.vector.tensor_tensor(x_mid[:], x_in[:], att[:].rearrange("p c h e -> p (c h e)"), ALU.add).then_inc(x_mid_a, 1)
                dve.wait_ge(x_mid_a, b + 1)
                assert step[0] == CHAIN_FULL, step

            def band_stage(b, m):
                link = chain_of(b_n, CHAIN_BAND, b)
                dve.wait_ge(x_moved, 16 * b + 16)
                moments(link, x_in, D)
                inverse_std(b_n.var, b_n.rstd, b)
                normalise(z, x_in, D).then_inc(b_n.done, 1)
                pieces(experts, m, "band", "pro0")
                dve.wait_ge(b_n.t, b + 1)
                nc.vector.tensor_copy(z_t[:], SQ[0][:, 0:T]).then_inc(b_n.t_sb, 1)
                dve.wait_ge(b_n.done, b + 1)
                link(nc.vector.tensor_tensor(xz[:], x_in[:], z[:].rearrange("p c d -> p (c d)"), ALU.add))
                pieces(experts, m, "band", "pro1")
                dve.wait_ge(s_ps, b + 1)
                link(nc.vector.tensor_tensor(s_band[:].rearrange("p c k -> p (c k)"), SK[0][:, 0:TC * T], const("band"), ALU.add))
                link(nc.vector.reduce_max(bmax[:], s_band[:], AX))
                nc.vector.tensor_scalar(nmax[:], bmax[:], -1.0, None, ALU.mult).then_inc(bmax_done, 1)
                dve.wait_ge(p_done, b + 1)
                link(nc.vector.reciprocal(r_band[:], sum_band[:]))
                dve.wait_ge(ra_ps, b + 1)
                for c in range(TC):
                    last = nc.vector.tensor_scalar(ra[:, c, :], SQ[0][:, c * D:(c + 1) * D], r_band[:, c:c + 1], 0.0,
                                                   ALU.mult, ALU.max)
                link(last)
                nc.vector.tensor_tensor(x_mid[:], xz[:], ra[:].rearrange("p c d -> p (c d)"), ALU.add).then_inc(x_mid_b, 1)
                dve.wait_ge(x_mid_b, b + 1)
                assert step[0] == CHAIN_BAND, step

            def causal_stage(n, b, m, base):
                link = chain_of(c_n, CHAIN_CAUSAL, n)
                moments(link, x_mid, D)
                inverse_std(c_n.var, c_n.rstd, n)
                link(nc.vector.tensor_tensor(sqr[:], rstd[:], rstd[:], ALU.mult))
                link(nc.vector.tensor_tensor(sqr[:], sqr[:], mv[:, :, 1], ALU.mult))
                nc.vector.tensor_scalar(ms[:], sqr[:], RMS_EPS, None, ALU.add).then_inc(c_ms, 1)
                link(normalise(z, x_mid, D))
                dve.wait_ge(c_rrms, n + 1)
                for c in range(TC):
                    last = nc.vector.tensor_scalar(zr[:, c, :], z[:, c, :], rrms[:, c:c + 1], None, ALU.mult)
                last.then_inc(c_n.done, 1)
                pieces(experts, m, "causal", "pro0")
                dve.wait_ge(c_n.t, n + 1)
                nc.vector.tensor_scalar(z_t[:], SQ[0][:, 0:T], col[:, 0:1], None, ALU.mult).then_inc(c_n.t_sb, 1)
                dve.wait_ge(lat_ps, n + 1)
                moments(link, SK[0], LAT)
                inverse_std(lat_var, lat_rstd, n)
                for c in range(TC):
                    last = nc.vector.tensor_scalar(lat_n[:, c, 0:LAT], SK[0][:, c * LAT:(c + 1) * LAT], mv[:, c, 0:1],
                                                   rstd[:, c:c + 1], ALU.subtract, ALU.mult)
                last.then_inc(lat_done, 1)

                def rope(ps, which, cos, sin):
                    nc.vector.tensor_tensor(rope_a[:], ps[:, 0:T], const(cos), ALU.mult)
                    link(nc.vector.tensor_tensor(rope_b[:], ps[:, T:2 * T], const(sin), ALU.mult))
                    link(nc.vector.tensor_tensor(qk[:, which, :], rope_a[:], rope_b[:], ALU.add))

                dve.wait_ge(lat_tps, n + 1)
                nc.vector.tensor_scalar(lat_t[:], SQ[0][0:LAT, 0:T], col[0:LAT, 2:3], col[0:LAT, 3:4], ALU.mult,
                                        ALU.add).then_inc(lat_tsb, 1)
                dve.wait_ge(q_ps, n + 1)
                rope(SQ[1], 0, "cos_q", "sin_q")
                pieces(experts, m, "causal", "pro1")
                dve.wait_ge(k_ps, n + 1)
                rope(SK[1], 1, "cos_k", "sin_k")
                split(causal, link, n, 2)
                pieces(experts, m, "causal", "pro2")
                mask_k1(causal, n)
                attend(causal, n, m)
                pieces(experts, m, "causal", "post")
                dve.wait_ge(y_ps, n + 1)
                link(nc.vector.tensor_tensor(y1[:].rearrange("p c d -> p (c d)"), SQ[1][:, 0:T], z[:].rearrange("p c d -> p (c d)"), ALU.add))
                link(nc.vector.tensor_tensor(sq[:], y1[:], y1[:], ALU.mult))
                link(nc.vector.reduce_sum(sqr[:], sq[:], AX))
                nc.vector.tensor_scalar(ms[:], sqr[:], 1.0 / D, RMS_EPS, ALU.mult, ALU.add).then_inc(y_ms, 1)
                dve.wait_ge(y_rrms, n + 1)
                for c in range(TC):
                    last = nc.vector.tensor_scalar(zr[:, c, :], y1[:, c, :], rrms[:, c:c + 1], None, ALU.mult)
                last.then_inc(xm_done, 1)
                dve.wait_ge(xm_tps, n + 1)
                nc.vector.tensor_scalar(xm_t[:], SQ[0][:, 0:T], col[:, 1:2], None, ALU.mult).then_inc(xm_tsb, 1)
                if base == 0 and m is not None:
                    dve.wait_ge(kept, b * 16)
                elif base and m is None:
                    dve.wait_ge(kept, 16 * B)
                elif base:
                    dve.wait_ge(stored, b * 16)
                link(nc.vector.tensor_tensor(acc[:], x_mid[:], y1[:].rearrange("p c d -> p (c d)"), ALU.add))
                dve.wait_ge(logit_ps, n + 1)
                link(nc.vector.tensor_tensor(logits[:], SQ[1][:, 0:TC * E].rearrange("p (c e) -> p c e", e=E),
                                             b_gate[:].unsqueeze(1).to_broadcast([P, TC, E]), ALU.add))
                link(nc.vector.reduce_max(lmax[:], logits[:], AX))
                link(nc.vector.tensor_tensor(ranked[:], logits[:], lmax[:].unsqueeze(2).to_broadcast([P, TC, E]), ALU.is_equal))
                link(nc.vector.tensor_tensor(ranked[:], ranked[:], const("priority").unsqueeze(1).to_broadcast([P, TC, E]), ALU.mult))
                link(nc.vector.reduce_max(rmax[:], ranked[:], AX))
                link(nc.vector.tensor_tensor(onehot[:], ranked[:], rmax[:].unsqueeze(2).to_broadcast([P, TC, E]), ALU.is_equal))
                assert step[0] == CHAIN_CAUSAL, step

            for base, first in ((0, full_stage), (B, band_stage)):
                first(0, None)
                causal_stage(base, 0, None, base)
                with dve.Fori(1, B, 1) as i:
                    first(i, base - 1 + i)
                    causal_stage(base + i, i, base - 1 + i, base)
                for k in range(PIECES):
                    experts(k, base + B - 1)

        @block.tensor
        def _(pe):
            pe.wait_ge(loaded, ALL_LOADED)
            pe.wait_ge(consts_ready, 2)

            def mm(o, lhs_t, rhs, start=True, stop=True):
                return nc.tensor.matmul(o, lhs_t, rhs, start=start, stop=stop)

            def experts(k, m):
                e, u = divmod(k, 3)
                ps = EX[k % 2]
                if u < 2:
                    if k == 0:
                        pe.wait_ge(xm_tsb, m + 1)
                    if u == 0 and e:
                        pe.wait_ge(relu, m * (2 * E) + 2 * e)
                    if u == 1 and e:
                        pe.wait_ge(combined, m * E + e)
                    for i in range(2):
                        j = 2 * u + i
                        last = mm(ps[:, i * T:(i + 1) * T], w_1[:, e, j * P:(j + 1) * P], xm_t[:])
                    last.then_inc(up, 1)
                else:
                    pe.wait_ge(relu, m * (2 * E) + 2 * e + 2)
                    for c in range(TC):
                        for j in range(J):
                            last = mm(ps[:, c * D:(c + 1) * D], hidden[:, e % 2, j, c * P:(c + 1) * P], w_2[:, e, j, :],
                                      start=j == 0, stop=j == J - 1)
                    last.then_inc(down, 1)

            def transpose2(dst, src, done):
                for c in range(TC):
                    last = nc.tensor.transpose(dst[:, c * P:(c + 1) * P], src(c), ident)
                last.then_inc(done, 1)

            def attend(core, n, m):
                def query_side(g, u):
                    c, v0, nv, keys = core.q_units[u]
                    idx = g * core.nq + u
                    ps = SQ[idx % 2]
                    if idx >= 2:
                        pe.wait_ge(core.maxed, n * (G * core.nq) + idx - 1)
                    if core.causal:
                        mm(ps[:], ident_b[:], masks_b[:, QM0 if c == 0 else QM1, :], stop=False)
                    mm(ps[:, 0:nv * keys].rearrange("p (v k) -> p v k", k=keys), q1[:, g, c * P:(c + 1) * P],
                       k1[:, g, v0:v0 + nv, 0:keys], start=not core.causal).then_inc(core.scores_q, 1)

                def transpose_max(g):
                    pe.wait_ge(core.maxed, n * (G * core.nq) + (g + 1) * core.nq)
                    if g >= 2:
                        pe.wait_ge(core.normed, n * G + g - 1)
                    for c in range(TC):
                        last = nc.tensor.transpose(tr_max[2 * QUAD:K2_ROWS, c * P:(c + 1) * P], maxima[:, g, c, :], ident_b[:])
                    last.then_inc(core.max_t, 1)

                def key_side(g, u):
                    kc, v0, nv, q0 = core.k_units[u]
                    idx = g * core.nk + u
                    ps = SK[idx % 2]
                    if u == 0:
                        pe.wait_ge(core.shift, n * G + g + 1)
                    if idx >= 2:
                        pe.wait_ge(core.probs, n * (G * core.nk) + idx - 1)
                    w = T - q0
                    if core.causal:
                        mm(ps[:], ident_b[:], masks_b[:, KM0 if kc == 0 else KM1, :], stop=False)
                    for i in range(nv):
                        v = v0 + i
                        o = ps[:, i * w:(i + 1) * w]
                        mm(o, k1[:, g, v, kc * P:(kc + 1) * P], q1[:, g, q0:T], start=not core.causal, stop=False)
                        last = mm(o, k2[0:K2_ROWS, g, v, kc * P:(kc + 1) * P], q2[0:K2_ROWS, g, q0:T], start=False,
                                  stop=not core.causal or i == nv - 1)
                    last.then_inc(core.scores_k, 1)

                def weigh(g):
                    pe.wait_ge(core.probs, n * (G * core.nk) + (g + 1) * core.nk)
                    if g:
                        pe.wait_ge(core.weighted_sb, n * G + g)
                    for kc in range(TC):
                        q0 = P if core.causal and kc else 0
                        for v in range(V):
                            last = mm(WT[v * QUAD:(v + 1) * QUAD, q0:T], values[:, kc, g * V + v, :],
                                      probs[:, g % 2, kc, v, q0:T], start=kc == 0, stop=kc == TC - 1)
                    last.then_inc(core.weighted, 1)

                def transpose_out(g):
                    pe.wait_ge(core.weighted_sb, n * G + g + 1)
                    pe.wait_ge(core.shift, n * G + min(g + 2, G))
                    if g:
                        pe.wait_ge(core.normed, n * G + g)
                    transpose2(TR, lambda c: wt_sb[:, g % 2, c * P:(c + 1) * P], core.out_t)

                pe.wait_ge(core.k1, n * V + V)
                query_side(0, 0)
                query_side(0, 1)
                for u in range(2, core.nq):
                    query_side(0, u)
                pe.wait_ge(core.k2, n * V + V)
                for g in range(G):
                    more = g + 1 < G
                    if more:
                        query_side(g + 1, 0)
                    transpose_max(g)
                    if more:
                        query_side(g + 1, 1)
                    key_side(g, 0)
                    key_side(g, 1)
                    if more:
                        for u in range(2, core.nq):
                            query_side(g + 1, u)
                    for u in range(2, core.nk):
                        key_side(g, u)
                    if g == 1:
                        pe.wait_ge(core.values, n + 1)
                    if g:
                        weigh(g - 1)
                        transpose_out(g - 1)
                weigh(G - 1)
                transpose_out(G - 1)

            def full_stage(b, m):
                pe.wait_ge(f_n.done, b + 1)
                transpose2(SQ[0], lambda c: z[:, c, :], f_n.t)
                pieces(experts, m, "full", "pro0")
                pieces(experts, m, "full", "pro1")
                attend(full, b, m)

            def band_stage(b, m):
                pe.wait_ge(b_n.done, b + 1)
                transpose2(SQ[0], lambda c: z[:, c, :], b_n.t)
                pieces(experts, m, "band", "pro0")
                pe.wait_ge(b_n.t_sb, b + 1)
                mm(SQ[1][:, 0:T], w_b[:], z_t[:]).then_inc(t_ps, 1)
                pieces(experts, m, "band", "pro1")
                pe.wait_ge(t_sb, b + 1)
                for c in range(TC):
                    last = mm(SK[0][:, c * T:(c + 1) * T], t_t[:, c * P:(c + 1) * P], z_t[:])
                last.then_inc(s_ps, 1)
                pe.wait_ge(p_done, b + 1)
                for kc in range(TC):
                    for c in range(TC):
                        last = nc.tensor.transpose(SK[1][:, kc * T + c * P:kc * T + (c + 1) * P],
                                                   p_band[:, c, kc * P:(kc + 1) * P], ident)
                last.then_inc(pt_ps, 1)
                pe.wait_ge(pt_sb, b + 1)
                for c in range(TC):
                    for kc in range(TC):
                        last = mm(SQ[0][:, c * D:(c + 1) * D], pt_band[:, kc, c * P:(c + 1) * P], z[:, kc, :],
                                  start=kc == 0, stop=kc == TC - 1)
                last.then_inc(ra_ps, 1)

            def causal_stage(n, b, m):
                pe.wait_ge(c_n.done, n + 1)
                transpose2(SQ[0], lambda c: zr[:, c, :], c_n.t)
                pieces(experts, m, "causal", "pro0")
                pe.wait_ge(c_n.t_sb, n + 1)
                for c in range(TC):
                    last = mm(SK[0][:, c * LAT:(c + 1) * LAT], z_t[:, c * P:(c + 1) * P], w_dkv[:])
                last.then_inc(lat_ps, 1)
                mm(SQ[1][:, 0:T], w_q[:], z_t[:])
                mm(SQ[1][:, T:2 * T], w_qr[:], z_t[:]).then_inc(q_ps, 1)
                pe.wait_ge(lat_done, n + 1)
                transpose2(SQ[0], lambda c: lat_n[:, c, :], lat_tps)
                pieces(experts, m, "causal", "pro1")
                pe.wait_ge(lat_tsb, n + 1)
                mm(SK[1][:, 0:T], w_uk[:], lat_t[:])
                mm(SK[1][:, T:2 * T], w_ukr[:], lat_t[:]).then_inc(k_ps, 1)
                for c in range(TC):
                    last = mm(SK[0][:, c * D:(c + 1) * D], lat_t[:, c * P:(c + 1) * P], w_uv[:])
                last.then_inc(v_ps, 1)
                pieces(experts, m, "causal", "pro2")
                attend(causal, n, m)
                pe.wait_ge(causal.normed, n * G + G)
                transpose2(SQ[0], lambda c: att[:, c, :, :].rearrange("p h e -> p (h e)"), att_tps)
                pieces(experts, m, "causal", "post")
                pe.wait_ge(att_tsb, n + 1)
                for c in range(TC):
                    last = mm(SQ[1][:, c * D:(c + 1) * D], att_t[:, c * P:(c + 1) * P], w_o[:])
                last.then_inc(y_ps, 1)
                pe.wait_ge(xm_done, n + 1)
                transpose2(SQ[0], lambda c: zr[:, c, :], xm_tps)
                pe.wait_ge(xm_tsb, n + 1)
                for c in range(TC):
                    last = mm(SQ[1][:, c * E:(c + 1) * E], xm_t[:, c * P:(c + 1) * P], w_gate[:])
                last.then_inc(logit_ps, 1)

            run(pe, full_stage, band_stage, causal_stage, experts, lambda base, b: None)


def constants():
    import numpy as np

    c = np.zeros((P, CST_COLS), np.float32)

    def put(name, a):
        c[:, CST[name][0]:CST[name][1]] = a

    r = np.arange(P)
    put("ident", np.eye(P, dtype=np.float32))
    later_key = np.where(r[None, :] > r[:, None], np.float32(-BIG), np.float32(0))
    zero = np.zeros((P, P), np.float32)
    put("qmask0", np.tile(later_key, (1, V)))
    put("qmask1", np.tile(np.concatenate([zero, later_key], 1), (1, 2)))
    put("kmask0", np.tile(np.concatenate([later_key.T, zero], 1), (1, 2)))
    put("kmask1", np.tile(later_key.T, (1, V)))
    k = np.arange(T)
    put("band", np.concatenate([np.where(np.abs(c0 * P + r[:, None] - k[None, :]) > BAND, np.float32(-BIG), np.float32(0))
                                for c0 in range(TC)], 1))
    half = HD // 2
    inv = (1.0 / np.float32(10000.0) ** (np.arange(half, dtype=np.float32) / np.float32(half))).astype(np.float32)
    ang = np.arange(T, dtype=np.float32)[:, None] * inv[None, :]
    dim = (r // G) % HD
    cos, sin = np.cos(ang).T[dim % half], np.sin(ang).T[dim % half] * np.where(dim < half, -1, 1)[:, None]
    scale = 1.0 / np.sqrt(HD)
    put("cos_q", cos * scale)
    put("sin_q", sin * scale)
    put("cos_k", cos)
    put("sin_k", sin)
    put("headmask", ((r % QUAD)[:, None] // HD == np.arange(V)[None, :]))
    put("shiftsel", -((r - 2 * QUAD)[:, None] == np.arange(V)[None, :]).astype(np.float32))
    put("priority", np.arange(E, 0, -1)[None, :])
    return c


def kernel(**inputs):
    import numpy as np
    import concourse.bacc as bacc
    from concourse.bass_utils import run_bass_kernel_spmd

    a = {k.replace("L0_", ""): np.asarray(v) for k, v in inputs.items()}
    order = np.arange(D).reshape(G, QUAD).T.reshape(-1)
    partner = (order // HD) * HD + (order % HD + HD // 2) % HD
    pad = np.zeros(D - LAT, np.float32)
    arrays = {
        "x": a["attn_a_x"], "wb": a["attn_b_W"],
        "wq": a["ffn_Wq"].T[:, order], "wqr": a["ffn_Wq"].T[:, partner],
        "wdkv": a["ffn_Wdkv"].T,
        "wuk": a["ffn_Wuk"].T[:, order], "wukr": a["ffn_Wuk"].T[:, partner], "wuv": a["ffn_Wuv"].T,
        "wo": a["ffn_Wo"].T, "gate": a["ffn_gate_w"].T,
        "w1": a["ffn_W1"].transpose(2, 0, 1),
        "w2": a["ffn_W2"].reshape(E, D, J, P).transpose(3, 0, 2, 1),
        "b1": a["ffn_b1"].reshape(E * J, P).T,
        "b2": np.broadcast_to(a["ffn_b2"][None], (P, E, D)),
        "gate_b": np.broadcast_to(a["ffn_gate_b"][None], (P, E)),
        "cols": np.stack([a["ffn_norm1_w"], a["ffn_norm2_w"], np.concatenate([a["ffn_ln_g"], pad]),
                          np.concatenate([a["ffn_ln_b"], pad])], 1),
        "cst": constants(),
    }
    arrays = {k: np.ascontiguousarray(v) for k, v in arrays.items()}
    nc = bacc.Bacc("TRN2", target_bir_lowering=False, num_devices=1)
    args = [nc.dram_tensor(f"in_{k}", v.shape, mybir.dt.from_np(v.dtype), kind="ExternalInput").ap()
            for k, v in arrays.items()]
    out = nc.dram_tensor("out_x", (B, T, D), F32, kind="ExternalOutput").ap()
    build(nc, *args, out)
    r = run_bass_kernel_spmd(nc, [{f"in_{k}": v for k, v in arrays.items()}], core_ids=[0])
    return r.results[0]["out_x"]
```

```python
from contextlib import ExitStack

import concourse.bass as bass
from concourse import mybir

F32 = mybir.dt.float32
BF16 = mybir.dt.bfloat16
ALU = mybir.AluOpType
ACT = mybir.ActivationFunctionType
AX = mybir.AxisListType.X

B, T, D = 32, 256, 128
P = 128
TC = T // P
H, HD = 16, 8
G, V = 4, 4
NP = H // 2
QUAD = 32
TERM = 2 * HD
Q_TERMS, K_TERMS = "hhmmlh", "hmhmhl"
ROWS = len(Q_TERMS) * TERM
ALL_ROWS = ROWS + 2
LAT = 64
E, HID = 4, 512
J = HID // P
PIECES = 3 * E
BAND = 64
LN_EPS, RMS_EPS = 1e-5, 1e-6
BIG = 1e30

CST, CST_COLS = {}, 0
for _name, _n in (("ident", P), ("qmask0", V * P), ("qmask1", 2 * T), ("kmask0", 2 * T), ("kmask1", V * P),
                  ("band", TC * T), ("cos_q", T), ("sin_q", T), ("cos_k", T), ("sin_k", T),
                  ("headmask", 2), ("shiftsel", 2), ("priority", E)):
    CST[_name] = (CST_COLS, CST_COLS + _n)
    CST_COLS += _n
QM0, QM1, KM0, KM1 = range(4)

SLOTS = 3 * G + 2
FIRST_A = ["zr_t m0", "lat m1", "m2", "q m3", "split_q lat_t m4", "k m5", "v split_k m6", "m7", "m8", "m9",
           "m10", "m11", "mask", "keep"]
FIRST_B = ["zr_t b_t m0", "lat b_w m1", "b_s m2", "b_soft q m3", "split_q lat_t m4", "b_pt k m5", "b_ra v split_k m6",
           "b_end m7", "m8", "m9", "m10", "m11", "mask", "keep"]
SECOND_A = ["x_load att_t", "y", "f_norm_a", "f_norm_b y_rms", "f_t xm", "f_centre f_split", "xm_t", "logit save",
            "route_a norm_a", "route_b norm_b", "norm_c", "", "f_mask", ""]
SECOND_B = ["x_load att_t", "y", "f_norm_a", "f_norm_b y_rms", "xm save", "norm_a", "xm_t norm_b", "logit norm_c",
            "route_a", "route_b", "", "", "", ""]
NORM = ("norm_a", "norm_b", "norm_c")
PRO = ("save", "zr_t", "lat", "q", "split_q", "lat_t", "k", "v", "split_k", "mask")
POST = ("att_t", "y", "y_rms", "xm", "xm_t", "logit", "route_a", "route_b")
NEXT = ("x_load", "f_norm_a", "f_norm_b", "f_t", "f_centre", "f_split", "f_mask")
BANDED = ("b_t", "b_w", "b_s", "b_soft", "b_pt", "b_ra", "b_end")


class Round:

    def __init__(self, s, like):
        self.s, self.like = s, like
        self.has_first, self.has_next = like < 2 * B, like + 1 < 2 * B
        self.has_core, self.has_post, self.has_experts = (d <= like < 2 * B + d for d in (1, 2, 3))
        self.first_full, self.next_full = like < B, like + 1 < B
        self.wide = not (self.has_first and self.first_full)
        self.first = s if self.first_full else s - B
        self.next = s + 1 if self.next_full else s + (1 - B)
        self.core, self.post, self.experts = s - 1, s - 2, s - 3

    def steps(self):
        def kept(name):
            if name[0] == "m" and name[1:].isdigit() or name == "keep":
                return self.has_experts
            if name in PRO:
                return self.has_core
            if name in POST:
                return self.has_post
            if name in NORM:
                return self.has_first
            if name in NEXT:
                return self.has_next
            return self.has_first and not self.first_full

        first = FIRST_A if self.first_full or not self.has_first else FIRST_B
        second = SECOND_A if self.next_full or not self.has_next else SECOND_B
        return [[[n for n in slot.split() if kept(n)] for slot in part] for part in (first, second)]


def rounds(engine, one):
    for lo, hi in ((0, 3), (3, B - 1), (B - 1, B + 3), (B + 3, 2 * B - 1), (2 * B - 1, 2 * B + 3)):
        if hi - lo > 4:
            with engine.Fori(lo, hi, 1) as s:
                one(Round(s, lo))
        else:
            for s in range(lo, hi):
                one(Round(s, s))


class Core:

    def __init__(self, kind, sem):
        self.kind, self.causal = kind, kind == "causal"
        if self.causal:
            self.q_units = [(0, 0, 2, P), (1, 0, 1, T), (1, 1, 1, T)]
            self.k_units = [(0, 0, 1, 0), (0, 1, 1, 0), (1, 0, 2, P)]
        else:
            self.q_units = [(c, i, 1, T) for c in range(TC) for i in (0, 1)]
            self.k_units = [(c, i, 1, 0) for c in range(TC) for i in (0, 1)]
        self.nq, self.nk = len(self.q_units), len(self.k_units)
        self.parts = 1 if kind == "full" else 2
        self.high, self.mid, self.low = (sem(f"{kind}_{n}_part") for n in ("high", "mid", "low"))
        self.stacked_q = sem(f"{kind}_q_stacked")
        self.stacked_k = sem(f"{kind}_k_stacked")
        self.masked = sem(f"{kind}_k_masked")
        self.values = sem(f"{kind}_values_ready")
        self.scores_q = sem(f"{kind}_scores_q")
        self.maxed = sem(f"{kind}_maxed")
        self.max_t = sem(f"{kind}_max_transposed")
        self.shift = sem(f"{kind}_shift_ready")
        self.scores_k = sem(f"{kind}_scores_k")
        self.probs = sem(f"{kind}_probs_ready")
        self.weighted = sem(f"{kind}_weighted")
        self.weighted_sb = sem(f"{kind}_weighted_sb")
        self.out_t = sem(f"{kind}_out_transposed")
        self.recip = sem(f"{kind}_denominators")
        self.normed = sem(f"{kind}_normed")


class Norm:

    def __init__(self, kind, sem):
        self.chain = sem(f"{kind}_dve_chain")
        self.var, self.rstd = sem(f"{kind}_var"), sem(f"{kind}_rstd")
        self.done = sem(f"{kind}_normalised")
        self.t, self.t_sb = sem(f"{kind}_norm_t"), sem(f"{kind}_norm_t_sb")


CHAIN_NEXT_FULL, CHAIN_NEXT_BAND, CHAIN_BAND, CHAIN_NORM, CHAIN_PRO, CHAIN_POST = 5, 2, 4, 4, 6, 7


def build(nc, x, wb, wq, wqr, wdkv, wuk, wukr, wuv, wo, gate, w1, w2, b1, b2, gate_b, cols, cst, out):
    with ExitStack() as ctx:
        def sb(name, shape, dt=F32):
            return ctx.enter_context(nc.sbuf_tensor(name, shape, dt))

        def sem(name):
            return ctx.enter_context(nc.semaphore(name))

        w_b = sb("w_b", [P, D])
        w_q, w_qr = sb("w_q", [P, D]), sb("w_qr", [P, D])
        w_dkv = sb("w_dkv", [P, LAT])
        w_uk, w_ukr, w_uv = sb("w_uk", [LAT, D]), sb("w_ukr", [LAT, D]), sb("w_uv", [LAT, D])
        w_o = sb("w_o", [P, D])
        w_gate = sb("w_gate", [P, E])
        w_1 = sb("w_1", [P, E, HID])
        w_2 = sb("w_2", [P, E, J, D])
        b_1 = sb("b_1", [P, E * J])
        b_2 = sb("b_2", [P, E, D])
        b_gate = sb("b_gate", [P, E])
        col = sb("col", [P, 4])
        c_sb = sb("c_sb", [P, CST_COLS])
        ident_b = sb("ident_b", [P, P], BF16)
        masks_b = sb("masks_b", [P, 4, 512], BF16)
        minus_half = sb("minus_half", [P, TC])

        def const(name):
            a, b = CST[name]
            return c_sb[:, a:b]

        ident = const("ident")

        x_all = sb("x_all", [P, B * T])
        x_in = sb("x_in", [P, T])
        x_mid = sb("x_mid", [P, T])
        z_f = sb("z_f", [P, TC, D])
        z = sb("z", [P, TC, D])
        xz_c = sb("xz_c", [P, T])
        z_old, xz_old = sb("z_old", [P, T]), sb("xz_old", [P, T])
        zr = sb("zr", [P, TC, D])
        z_t = sb("z_t", [P, T])
        stats = sb("stats", [P, TC, 6])
        mv = sb("mv", [P, TC, 2])
        var_eps, rstd = sb("var_eps", [P, TC]), sb("rstd", [P, TC])
        sqr = sb("sqr", [P, TC])
        ms, rrms = sb("ms", [P, TC]), sb("rrms", [P, TC])
        lat_sb = sb("lat_sb", [P, TC * LAT])
        lat_n = sb("lat_n", [P, TC, P])
        lat_t = sb("lat_t", [LAT, T])
        rope_a, rope_b = sb("rope_a", [P, T]), sb("rope_b", [P, T])
        mean = sb("mean", [P, 2])
        spacer = sb("spacer", [P, 1])
        qk_f = sb("qk_f", [P, 1, T])
        qk_c = sb("qk_c", [P, 2, T])
        rest = sb("rest", [P, 2, T])

        def stack_buffers(kind, n):
            parts = {x: sb(f"part_{x}_{kind}", [P, n, T], BF16) for x in "hml"}
            return (parts, sb(f"q_stack_{kind}", [P, NP, T], BF16), sb(f"k_raw_{kind}", [ROWS, NP, T], BF16),
                    sb(f"k_stack_{kind}", [P, NP, 2, T], BF16))

        f_buf, c_buf = stack_buffers("full", 1), stack_buffers("causal", 2)
        maxima = sb("maxima", [P, NP, TC, 2], BF16)
        probs = sb("probs", [P, 2, TC, V, T])
        values_f, values_c = sb("values_f", [P, TC, H, QUAD]), sb("values_c", [P, TC, H, QUAD])
        wt_sb = sb("wt_sb", [P, 2, T])
        rsum = sb("rsum", [P, G, TC, V])
        att_f, att_c = sb("att_f", [P, TC, H, HD]), sb("att_c", [P, TC, H, HD])
        att_t = sb("att_t", [P, T])
        y1 = sb("y1", [P, TC, D])
        sq = sb("sq", [P, TC, D])
        xm = sb("xm", [P, TC, D])
        xm_t = sb("xm_t", [P, T])
        logits = sb("logits", [P, TC, E])
        lmax, rmax = sb("lmax", [P, TC]), sb("rmax", [P, TC])
        ranked = sb("ranked", [P, TC, E])
        onehot = sb("onehot", [P, TC, E])
        hidden = sb("hidden", [P, 2, J, T])
        y_b = sb("y_b", [P, TC, D])
        acc = sb("acc", [P, T])
        t_t = sb("t_t", [P, T])
        s_band = sb("s_band", [P, TC, T])
        p_band, pt_band = sb("p_band", [P, TC, T]), sb("pt_band", [P, TC, T])
        bmax, nmax = sb("bmax", [P, TC]), sb("nmax", [P, TC])
        sum_band, r_band = sb("sum_band", [P, TC]), sb("r_band", [P, TC])
        z_bt = sb("z_bt", [P, T])
        xz, ra = sb("xz", [P, T]), sb("ra", [P, TC, D])

        bank = [ctx.enter_context(nc.psum_tensor(f"bank{i}", [P, 512], F32)) for i in range(8)]
        SQ, SK, WT, TR, SIDE, EX = bank[0:2], bank[2:4], bank[4], bank[5], bank[6], bank[7]
        tr_max = TR[:, 256:512].bitcast(BF16)

        loaded, consts_ready, zeroed, ones_set = sem("weights_loaded"), sem("consts_ready"), sem("zeroed"), sem("ones_set")
        x_loaded, x_moved = sem("x_loaded"), sem("x_moved")
        full, causal = Core("full", sem), Core("causal", sem)
        f_n, c_n, b_n = Norm("full", sem), Norm("causal", sem), Norm("band", sem)
        norm_chain = sem("norm_dve_chain")
        post_chain, band_chain = sem("post_dve_chain"), sem("banded_dve_chain")
        f_buf_of = {"full": f_buf, "causal": c_buf}
        x_mid_a, x_mid_b = sem("x_mid_full"), sem("x_mid_banded")
        centred = sem("centred")
        saved, xz_done, lat_copied, q_read, k_read = (sem(n) for n in (
            "z_saved", "x_plus_z", "latent_copied", "q_read", "k_read"))
        acc_ready, routed, zr_done, y1_done = sem("acc_ready"), sem("routed"), sem("zr_ready"), sem("y1_ready")
        c_ms, c_rrms = sem("z_mean_square"), sem("z_inverse_rms")
        lat_ps, lat_var, lat_rstd = sem("latent_psum"), sem("latent_var"), sem("latent_rstd")
        lat_done, lat_tps, lat_tsb = sem("latent_normalised"), sem("latent_t_psum"), sem("latent_t_sb")
        q_ps, k_ps, v_ps = sem("q_psum"), sem("k_psum"), sem("v_psum")
        att_tps, att_tsb, y_ps = sem("att_t_psum"), sem("att_t_sb"), sem("att_projected")
        y_ms, y_rrms = sem("y_mean_square"), sem("y_inverse_rms")
        xm_done, xm_tps, xm_tsb, logit_ps = sem("xm_ready"), sem("xm_t_psum"), sem("xm_t_sb"), sem("logits_psum")
        t_ps, t_sb, s_ps, bmax_done = sem("band_t_psum"), sem("band_t_sb"), sem("band_scores"), sem("band_max")
        p_done, pt_ps, pt_sb, ra_ps = sem("band_probs"), sem("band_pt_psum"), sem("band_pt_sb"), sem("band_weighted")
        up, relu, down = sem("expert_up"), sem("expert_relu"), sem("expert_down")
        biased, combined = sem("expert_biased"), sem("expert_combined")
        kept, stored = sem("acc_kept"), sem("stored")

        x_d = x.rearrange("b (c p) d -> b p c d", p=P)
        out_d = out.rearrange("b (c p) d -> b p c d", p=P)

        LOADS = [(w_b[:], wb), (w_q[:], wq), (w_qr[:], wqr), (w_dkv[:], wdkv), (w_uk[:], wuk), (w_ukr[:], wukr),
                 (w_uv[:], wuv), (w_o[:], wo), (w_gate[:], gate), (w_1[:], w1), (w_2[:], w2), (b_1[:], b1),
                 (b_2[:], b2), (b_gate[:], gate_b), (col[:], cols), (c_sb[:], cst)]
        ALL_LOADED = 16 * len(LOADS)

        def expert_bank(k, wide):
            return WT if wide and k % 2 else EX

        block = ctx.enter_context(nc.Block())

        @block.sync
        def _(sp):
            for dst, src in LOADS:
                sp.dma_start(dst, src).then_inc(loaded, 16)

            def stack(core, buf, n, which, sides):
                parts, q_stack, k_raw, _ = buf
                count = n * core.parts + which + 1
                for part, ready in (("h", core.high), ("m", core.mid), ("l", core.low)):
                    sp.wait_ge(ready, count)
                    for terms, dst, done, side in ((Q_TERMS, q_stack, core.stacked_q, "q"), (K_TERMS, k_raw, core.stacked_k, "k")):
                        for t, of in enumerate(terms):
                            if of == part and side in sides:
                                sp.dma_start(dst[t * TERM:(t + 1) * TERM, :, :].rearrange("r g t -> r (g t)"),
                                             parts[part][:, which, :]).then_inc(done, 16)

            def one(r):
                def step(name):
                    if name == "split_q":
                        stack(causal, c_buf, r.core, 0, "q")
                    elif name == "split_k":
                        stack(causal, c_buf, r.core, 1, "k")
                    elif name == "f_split":
                        stack(full, f_buf, r.next, 0, "qk")
                    elif name == "x_load" and r.next_full:
                        if r.like >= 0:
                            sp.wait_ge(x_mid_a, r.next)
                        load_x(r.next)
                    elif name == "x_load":
                        if r.like + 1 == B:
                            sp.wait_ge(x_mid_a, B)
                        else:
                            sp.wait_ge(x_mid_b, r.next)
                        sp.wait_ge(kept, 16 * (B - 3) if r.like + 1 < B + 3 else 16 * B)
                        sp.dma_start(x_in[:], x_all[:, bass.ds(r.next * T, T)]).then_inc(x_moved, 16)
                    elif name == "keep":
                        sp.wait_ge(combined, r.experts * E + E)
                        if r.like - 3 < B:
                            sp.dma_start(x_all[:, bass.ds(r.experts * T, T)], acc[:]).then_inc(kept, 16)
                        else:
                            sp.dma_start(out_d[bass.ds(r.experts - B, 1), :, :, :].rearrange("o p c d -> (o p) c d"),
                                         acc[:].rearrange("p (c d) -> p c d", c=TC)).then_inc(stored, 16)

                for part in r.steps():
                    for slot in part:
                        for name in slot:
                            step(name)

            def load_x(b):
                sp.dma_start(x_in[:].rearrange("p (c d) -> p c d", c=TC),
                             x_d[bass.ds(b, 1), :, :, :].rearrange("o p c d -> (o p) c d")).then_inc(x_loaded, 16)

            load_x(0)
            stack(full, f_buf, 0, 0, "qk")
            rounds(sp, one)
            sp.wait_ge(stored, 16 * B)

        @block.gpsimd
        def _(pool):
            for tensor, value in ((values_f, 0.0), (values_c, 0.0), (lat_n, 0.0), (minus_half, -0.5)):
                nc.gpsimd.memset(tensor[:], value).then_inc(zeroed, 1)
            pool.wait_ge(zeroed, 4)
            for tensor in (values_f, values_c):
                nc.gpsimd.memset(tensor[:, :, :, HD:HD + 1], 1.0).then_inc(ones_set, 1)
            pool.wait_ge(ones_set, 2)

            def inverse_root(dst, src, ready, done, n):
                pool.wait_ge(ready, n + 1)
                nc.gpsimd.tensor_tensor(dst[:], src[:], minus_half[:], ALU.pow).then_inc(done, 1)

            def one(r):
                def step(name):
                    if name == "norm_a":
                        inverse_root(rstd, var_eps, c_n.var, c_n.rstd, r.s)
                    elif name == "norm_b":
                        inverse_root(rrms, ms, c_ms, c_rrms, r.s)
                        pool.wait_ge(c_n.done, r.s + 1)
                        nc.gpsimd.tensor_tensor(xz_c[:], x_mid[:], z[:].rearrange("p c d -> p (c d)"), ALU.add).then_inc(xz_done, 1)
                    elif name == "lat":
                        inverse_root(rstd, var_eps, lat_var, lat_rstd, r.core)
                    elif name == "y_rms":
                        inverse_root(rrms, ms, y_ms, y_rrms, r.post)
                    elif name == "f_norm_a":
                        which = f_n if r.next_full else b_n
                        inverse_root(rstd, var_eps, which.var, which.rstd, r.next)

                for part in r.steps():
                    for slot in part:
                        for name in slot:
                            step(name)

            inverse_root(rstd, var_eps, f_n.var, f_n.rstd, 0)
            rounds(pool, one)

        @block.scalar
        def _(act):
            act.wait_ge(loaded, ALL_LOADED)
            act.wait_ge(ones_set, 2)

            def experts(k, m, wide):
                e, u = divmod(k, 3)
                if u == 2:
                    return
                ps = expert_bank(k, wide)
                act.wait_ge(up, m * (2 * E) + 2 * e + u + 1)
                if e >= 2 and u == 0:
                    act.wait_ge(down, m * E + e - 1)
                for i in range(2):
                    j = 2 * u + i
                    last = nc.scalar.activation(hidden[:, e % 2, j, :], ps[:, i * T:(i + 1) * T], ACT.Relu,
                                                bias=b_1[:, e * J + j:e * J + j + 1])
                last.then_inc(relu, 1)

            def copy_values_full(b):
                act.wait_ge(f_n.done, b + 1)
                for c in range(TC):
                    last = nc.scalar.copy(values_f[:, c, :, 0:HD].rearrange("p (g f) e -> p g f e", g=NP),
                                          z_f[:, c, :].rearrange("p (f e g) -> p g f e", f=2, e=HD))
                last.then_inc(full.values, 1)

            def attend(core, buf, n, slot):
                q_stack = buf[1]

                def copy_weighted(g):
                    act.wait_ge(core.weighted, n * G + g + 1)
                    nc.scalar.copy(wt_sb[:, g % 2, :], WT[:, 0:T]).then_inc(core.weighted_sb, 1)

                def exponentials(g, u):
                    kc, i0, pairs, q0 = core.k_units[u]
                    idx = g * core.nk + u
                    act.wait_ge(core.scores_k, n * (G * core.nk) + idx + 1)
                    if u == 0 and g >= 2:
                        act.wait_ge(core.weighted, n * G + g - 1)
                    w = T - q0
                    nc.scalar.activation(probs[:, g % 2, kc, 2 * i0:2 * (i0 + pairs), q0:T],
                                         SK[idx % 2][:, 0:2 * pairs * w].rearrange("p (v q) -> p v q", q=w),
                                         ACT.Exp).then_inc(core.probs, 1)

                slot(0)
                for g in range(G):
                    slot(3 * g + 1)
                    act.wait_ge(core.max_t, n * G + g + 1)
                    nc.scalar.copy(q_stack[ROWS:ALL_ROWS, 2 * g:2 * g + 2, :],
                                   tr_max[ROWS:ALL_ROWS, :].rearrange("p (i q) -> p i q", i=2)).then_inc(core.shift, 1)
                    if g:
                        copy_weighted(g - 1)
                    exponentials(g, 0)
                    exponentials(g, 1)
                    slot(3 * g + 2)
                    for u in range(2, core.nk):
                        exponentials(g, u)
                    slot(3 * g + 3)
                copy_weighted(G - 1)
                slot(SLOTS - 1)

            def one(r):
                def step(name):
                    if name[1:].isdigit():
                        experts(int(name[1:]), r.experts, r.wide)
                    elif name == "save":
                        act.wait_ge(xz_done, r.core + 1)
                        if r.has_post:
                            act.wait_ge(acc_ready, r.post + 1)
                        nc.scalar.copy(z_old[:], z[:].rearrange("p c d -> p (c d)"))
                        nc.scalar.copy(xz_old[:], xz_c[:]).then_inc(saved, 1)
                    elif name == "zr_t":
                        act.wait_ge(c_n.t, r.core + 1)
                        nc.scalar.activation(z_t[:], SIDE[:, 0:T], ACT.Copy, scale=col[:, 0:1]).then_inc(c_n.t_sb, 1)
                    elif name == "lat":
                        act.wait_ge(lat_ps, r.core + 1)
                        nc.scalar.copy(lat_sb[:], SIDE[:, 0:TC * LAT]).then_inc(lat_copied, 1)
                    elif name == "lat_t":
                        act.wait_ge(lat_tps, r.core + 1)
                        nc.scalar.activation(lat_t[:], SIDE[0:LAT, 0:T], ACT.Identity, scale=col[0:LAT, 2:3],
                                             bias=col[0:LAT, 3:4]).then_inc(lat_tsb, 1)
                    elif name == "v":
                        act.wait_ge(v_ps, r.core + 1)
                        for c in range(TC):
                            last = nc.scalar.copy(values_c[:, c, :, 0:HD],
                                                  SIDE[:, c * D:(c + 1) * D].rearrange("p (h e) -> p h e", e=HD))
                        last.then_inc(causal.values, 1)
                    elif name == "att_t":
                        act.wait_ge(att_tps, r.post + 1)
                        nc.scalar.copy(att_t[:], SIDE[:, 0:T]).then_inc(att_tsb, 1)
                    elif name == "xm_t":
                        act.wait_ge(xm_tps, r.post + 1)
                        nc.scalar.activation(xm_t[:], SIDE[:, 0:T], ACT.Copy, scale=col[:, 1:2]).then_inc(xm_tsb, 1)
                    elif name == "f_split":
                        copy_values_full(r.next)
                    elif name == "b_t":
                        act.wait_ge(b_n.t, r.first + 1)
                        nc.scalar.copy(z_bt[:], SQ[0][:, 0:T]).then_inc(b_n.t_sb, 1)
                    elif name == "b_w":
                        act.wait_ge(t_ps, r.first + 1)
                        nc.scalar.copy(t_t[:], SQ[1][:, 0:T]).then_inc(t_sb, 1)
                    elif name == "b_soft":
                        act.wait_ge(bmax_done, r.first + 1)
                        for c in range(TC):
                            last = nc.scalar.activation(p_band[:, c, :], s_band[:, c, :], ACT.Exp, bias=nmax[:, c:c + 1],
                                                        accum_out=sum_band[:, c:c + 1])
                        last.then_inc(p_done, 1)
                    elif name == "b_pt":
                        act.wait_ge(pt_ps, r.first + 1)
                        nc.scalar.copy(pt_band[:].rearrange("p c q -> p (c q)"), SK[1][:, 0:TC * T]).then_inc(pt_sb, 1)

                first, second = r.steps()

                def slots(part):
                    def slot(i):
                        for name in part[i]:
                            step(name)
                    return slot

                if r.has_first and r.first_full:
                    attend(full, f_buf, r.first, slots(first))
                else:
                    for i in range(SLOTS):
                        slots(first)(i)
                if r.has_core:
                    attend(causal, c_buf, r.core, slots(second))
                else:
                    for i in range(SLOTS):
                        slots(second)(i)

            copy_values_full(0)
            rounds(act, one)

        @block.vector
        def _(dve):
            dve.wait_ge(loaded, ALL_LOADED)
            dve.wait_ge(ones_set, 2)
            nc.vector.tensor_copy(ident_b[:], ident)
            for i, name in enumerate(("qmask0", "qmask1", "kmask0", "kmask1")):
                nc.vector.tensor_copy(masks_b[:, i, :], const(name))
            for _, _, _, k_stack in (f_buf, c_buf):
                last = nc.vector.memset(k_stack[ROWS:ALL_ROWS, :, :, :], 1.0)
            last.then_inc(consts_ready, 1)
            dve.wait_ge(consts_ready, 1)
            for _, _, _, k_stack in (f_buf, c_buf):
                for v in range(2):
                    last = nc.vector.tensor_scalar(k_stack[ROWS:ALL_ROWS, :, v, :], k_stack[ROWS:ALL_ROWS, :, v, :],
                                                   const("shiftsel")[ROWS:ALL_ROWS, v:v + 1], None, ALU.mult)
            last.then_inc(consts_ready, 1)

            done = {}

            def chain_of(chain, per, n, begin=False, end=False):
                key = chain.name
                if begin:
                    done[key] = 0

                def link(ins):
                    done[key] += 1
                    assert done[key] <= per, (key, per)
                    ins.then_inc(chain, 1)
                    dve.wait_ge(chain, n * per + done[key])
                return link

            def ended(chain, per):
                assert done[chain.name] == per, (chain.name, done[chain.name], per)

            def experts(k, m, wide):
                e, u = divmod(k, 3)
                if u != 2:
                    return
                dve.wait_ge(down, m * E + e + 1)
                if e:
                    dve.wait_ge(combined, m * E + e)
                nc.vector.tensor_tensor(y_b[:], expert_bank(k, wide)[:, 0:T].rearrange("p (c d) -> p c d", c=TC),
                                        b_2[:, e:e + 1, :].to_broadcast([P, TC, D]), ALU.add).then_inc(biased, 1)
                dve.wait_ge(biased, m * E + e + 1)
                for c in range(TC):
                    last = nc.vector.scalar_tensor_tensor(acc[:, c * D:(c + 1) * D], y_b[:, c, :], onehot[:, c, e:e + 1],
                                                          acc[:, c * D:(c + 1) * D], ALU.mult, ALU.add)
                last.then_inc(combined, 1)

            def moments(link, src, width, ready):
                for c in range(TC):
                    last = nc.vector.bn_stats(stats[:, c, :], src[:, c * width:(c + 1) * width])
                link(last)
                nc.vector.memset(spacer[:], 0.0)
                for c in range(TC):
                    last = nc.vector.bn_aggr(mv[:, c, :], stats[:, c, :])
                link(last)
                nc.vector.tensor_scalar(var_eps[:], mv[:, :, 1], LN_EPS, None, ALU.add).then_inc(ready, 1)

            def normalise(dst, src, width):
                for c in range(TC):
                    last = nc.vector.tensor_scalar(dst[:, c, 0:width], src[:, c * width:(c + 1) * width], mv[:, c, 0:1],
                                                   rstd[:, c:c + 1], ALU.subtract, ALU.mult)
                return last

            def normalise_full(b):
                dve.wait_ge(f_n.rstd, b + 1)
                for c in range(TC):
                    last = nc.vector.tensor_scalar(z_f[:, c, :].rearrange("p (r g) -> p g r", g=NP),
                                                   x_in[:, c * D:(c + 1) * D].rearrange("p (g r) -> p g r", g=NP),
                                                   mv[:, c, 0:1], rstd[:, c:c + 1], ALU.subtract, ALU.mult)
                last.then_inc(f_n.done, 1)

            def centre(link, b):
                dve.wait_ge(f_n.t, b + 1)
                link(nc.vector.reduce_sum(mean[:, 0:1], SIDE[:, 0:T], AX))
                link(nc.vector.tensor_scalar(mean[:, 1:2], mean[:, 0:1], 1.0 / T, None, ALU.mult))
                nc.vector.tensor_scalar(qk_f[:, 0, :], SIDE[:, 0:T], mean[:, 1:2], None, ALU.subtract).then_inc(centred, 1)
                dve.wait_ge(centred, b + 1)

            def split(core, buf, link, n, which, src):
                parts, count = buf[0], n * core.parts + which + 1
                high, mid, low = (parts[x][:, which, :] for x in "hml")
                nc.vector.tensor_copy(high, src[:, which, :]).then_inc(core.high, 1)
                dve.wait_ge(core.high, count)
                link(nc.vector.tensor_tensor(rest[:, which, :], src[:, which, :], high, ALU.subtract))
                nc.vector.tensor_copy(mid, rest[:, which, :]).then_inc(core.mid, 1)
                dve.wait_ge(core.mid, count)
                nc.vector.tensor_tensor(low, rest[:, which, :], mid, ALU.subtract).then_inc(core.low, 1)

            def mask(core, buf, n):
                _, _, k_raw, k_stack = buf
                dve.wait_ge(core.stacked_k, n * (16 * len(K_TERMS)) + 16 * len(K_TERMS))
                for v in range(2):
                    last = nc.vector.tensor_scalar(k_stack[0:ROWS, :, v, :], k_raw[:], const("headmask")[0:ROWS, v:v + 1],
                                                   None, ALU.mult)
                last.then_inc(core.masked, 1)

            def attend(core, att, n, slot):
                def row_max(g, u):
                    c, i0, pairs, keys = core.q_units[u]
                    idx = g * core.nq + u
                    dve.wait_ge(core.scores_q, n * (G * core.nq) + idx + 1)
                    nc.vector.reduce_max(maxima[:, 2 * g + i0:2 * g + i0 + pairs, c, :],
                                         SQ[idx % 2][:, 0:2 * pairs * keys].rearrange("p (i v k) -> p i v k", i=pairs, k=keys),
                                         AX).then_inc(core.maxed, 1)

                def divide(g):
                    dve.wait_ge(core.out_t, n * G + g + 1)
                    o = TR[:, 0:T].rearrange("p (c v r) -> p c v r", c=TC, r=QUAD)
                    nc.vector.reciprocal(rsum[:, g, :, :], o[:, :, :, HD]).then_inc(core.recip, 1)
                    dve.wait_ge(core.recip, n * G + g + 1)
                    nc.vector.tensor_tensor(att[:, :, g * V:(g + 1) * V, :], o[:, :, :, 0:HD],
                                            rsum[:, g, :, :].unsqueeze(3).to_broadcast([P, TC, V, HD]), ALU.mult).then_inc(core.normed, 1)

                row_max(0, 0)
                row_max(0, 1)
                slot(0)
                for u in range(2, core.nq):
                    row_max(0, u)
                for g in range(G):
                    more = g + 1 < G
                    if more:
                        row_max(g + 1, 0)
                    slot(3 * g + 1)
                    if more:
                        row_max(g + 1, 1)
                    slot(3 * g + 2)
                    if more:
                        for u in range(2, core.nq):
                            row_max(g + 1, u)
                    if g:
                        divide(g - 1)
                    slot(3 * g + 3)
                slot(SLOTS - 1)
                divide(G - 1)

            def one(r):
                pro = chain_of(c_n.chain, CHAIN_PRO, r.core)
                post = chain_of(post_chain, CHAIN_POST, r.post)
                norm = chain_of(norm_chain, CHAIN_NORM, r.s)
                band = chain_of(band_chain, CHAIN_BAND, r.first)
                if r.next_full:
                    nxt = chain_of(f_n.chain, CHAIN_NEXT_FULL, r.next)
                else:
                    nxt = chain_of(b_n.chain, CHAIN_NEXT_BAND, r.next)

                def step(name):
                    if name[1:].isdigit():
                        experts(int(name[1:]), r.experts, r.wide)
                    elif name == "lat":
                        done[c_n.chain.name] = 0
                        dve.wait_ge(lat_copied, r.core + 1)
                        moments(pro, lat_sb, LAT, lat_var)
                    elif name == "q":
                        dve.wait_ge(lat_rstd, r.core + 1)
                        normalise(lat_n, lat_sb, LAT).then_inc(lat_done, 1)
                        dve.wait_ge(q_ps, r.core + 1)
                        rope(0, "cos_q", "sin_q", q_read, r.core)
                    elif name == "split_q":
                        split(causal, c_buf, pro, r.core, 0, qk_c)
                    elif name == "k":
                        dve.wait_ge(k_ps, r.core + 1)
                        rope(1, "cos_k", "sin_k", k_read, r.core)
                    elif name == "split_k":
                        split(causal, c_buf, pro, r.core, 1, qk_c)
                        ended(c_n.chain, CHAIN_PRO)
                    elif name == "mask":
                        mask(causal, c_buf, r.core)
                    elif name == "y":
                        done[post_chain.name] = 0
                        dve.wait_ge(y_ps, r.post + 1)
                        nc.vector.tensor_tensor(y1[:].rearrange("p c d -> p (c d)"), SIDE[:, 0:T], z_old[:], ALU.add).then_inc(y1_done, 1)
                        if 1 <= r.like - 2 <= B:
                            dve.wait_ge(kept, 16 * r.post)
                        elif r.like - 2 > B:
                            dve.wait_ge(stored, 16 * (r.post - B))
                        nc.vector.tensor_tensor(acc[:], SIDE[:, 0:T], xz_old[:], ALU.add).then_inc(acc_ready, 1)
                        dve.wait_ge(y1_done, r.post + 1)
                        post(nc.vector.tensor_tensor(sq[:], y1[:], y1[:], ALU.mult))
                        post(nc.vector.reduce_sum(sqr[:], sq[:], AX))
                        nc.vector.tensor_scalar(ms[:], sqr[:], 1.0 / D, RMS_EPS, ALU.mult, ALU.add).then_inc(y_ms, 1)
                    elif name == "xm":
                        dve.wait_ge(y_rrms, r.post + 1)
                        for c in range(TC):
                            last = nc.vector.tensor_scalar(xm[:, c, :], y1[:, c, :], rrms[:, c:c + 1], None, ALU.mult)
                        last.then_inc(xm_done, 1)
                    elif name == "route_a":
                        dve.wait_ge(logit_ps, r.post + 1)
                        post(nc.vector.tensor_tensor(logits[:], SIDE[:, 0:TC * E].rearrange("p (c e) -> p c e", e=E),
                                                     b_gate[:].unsqueeze(1).to_broadcast([P, TC, E]), ALU.add))
                        post(nc.vector.reduce_max(lmax[:], logits[:], AX))
                        post(nc.vector.tensor_tensor(ranked[:], logits[:], lmax[:].unsqueeze(2).to_broadcast([P, TC, E]), ALU.is_equal))
                    elif name == "route_b":
                        post(nc.vector.tensor_tensor(ranked[:], ranked[:], const("priority").unsqueeze(1).to_broadcast([P, TC, E]), ALU.mult))
                        post(nc.vector.reduce_max(rmax[:], ranked[:], AX))
                        nc.vector.tensor_tensor(onehot[:], ranked[:], rmax[:].unsqueeze(2).to_broadcast([P, TC, E]), ALU.is_equal).then_inc(routed, 1)
                        dve.wait_ge(routed, r.post + 1)
                        ended(post_chain, CHAIN_POST)
                    elif name == "norm_a":
                        done[norm_chain.name] = 0
                        moments(norm, x_mid, D, c_n.var)
                    elif name == "norm_b":
                        dve.wait_ge(c_n.rstd, r.s + 1)
                        norm(nc.vector.tensor_tensor(sqr[:], rstd[:], rstd[:], ALU.mult))
                        norm(nc.vector.tensor_tensor(sqr[:], sqr[:], mv[:, :, 1], ALU.mult))
                        nc.vector.tensor_scalar(ms[:], sqr[:], RMS_EPS, None, ALU.add).then_inc(c_ms, 1)
                        if r.has_core:
                            dve.wait_ge(saved, r.core + 1)
                        normalise(z, x_mid, D).then_inc(c_n.done, 1)
                        dve.wait_ge(c_n.done, r.s + 1)
                        ended(norm_chain, CHAIN_NORM)
                    elif name == "norm_c":
                        dve.wait_ge(c_rrms, r.s + 1)
                        for c in range(TC):
                            last = nc.vector.tensor_scalar(zr[:, c, :], z[:, c, :], rrms[:, c:c + 1], None, ALU.mult)
                        last.then_inc(zr_done, 1)
                    elif name == "f_norm_a":
                        if r.next_full:
                            dve.wait_ge(x_loaded, 16 * r.next + 16)
                            done[f_n.chain.name] = 0
                            moments(nxt, x_in, D, f_n.var)
                        else:
                            dve.wait_ge(x_moved, 16 * r.next + 16)
                            done[b_n.chain.name] = 0
                            moments(nxt, x_in, D, b_n.var)
                            ended(b_n.chain, CHAIN_NEXT_BAND)
                    elif name == "f_norm_b":
                        if r.next_full:
                            normalise_full(r.next)
                        else:
                            dve.wait_ge(b_n.rstd, r.next + 1)
                            normalise(z_f, x_in, D).then_inc(b_n.done, 1)
                    elif name == "f_centre":
                        centre(nxt, r.next)
                    elif name == "f_split":
                        split(full, f_buf, nxt, r.next, 0, qk_f)
                        ended(f_n.chain, CHAIN_NEXT_FULL)
                    elif name == "f_mask":
                        mask(full, f_buf, r.next)
                    elif name == "b_t":
                        done[band_chain.name] = 0
                        dve.wait_ge(b_n.done, r.first + 1)
                        nc.vector.tensor_tensor(xz[:], x_in[:], z_f[:].rearrange("p c d -> p (c d)"), ALU.add)
                    elif name == "b_s":
                        dve.wait_ge(s_ps, r.first + 1)
                        band(nc.vector.tensor_tensor(s_band[:].rearrange("p c k -> p (c k)"), SK[0][:, 0:TC * T], const("band"), ALU.add))
                        band(nc.vector.reduce_max(bmax[:], s_band[:], AX))
                        nc.vector.tensor_scalar(nmax[:], bmax[:], -1.0, None, ALU.mult).then_inc(bmax_done, 1)
                    elif name == "b_ra":
                        dve.wait_ge(p_done, r.first + 1)
                        band(nc.vector.reciprocal(r_band[:], sum_band[:]))
                        dve.wait_ge(ra_ps, r.first + 1)
                        for c in range(TC):
                            last = nc.vector.tensor_scalar(ra[:, c, :], SQ[0][:, c * D:(c + 1) * D], r_band[:, c:c + 1], 0.0,
                                                           ALU.mult, ALU.max)
                        band(last)
                    elif name == "b_end":
                        if r.has_core:
                            dve.wait_ge(xz_done, r.core + 1)
                        nc.vector.tensor_tensor(x_mid[:], xz[:], ra[:].rearrange("p c d -> p (c d)"), ALU.add).then_inc(x_mid_b, 1)
                        dve.wait_ge(x_mid_b, r.first + 1)
                        ended(band_chain, CHAIN_BAND)

                def rope(which, cos, sin, read, n):
                    nc.vector.tensor_tensor(rope_a[:], SIDE[:, 0:T], const(cos), ALU.mult)
                    nc.vector.tensor_tensor(rope_b[:], SIDE[:, T:2 * T], const(sin), ALU.mult).then_inc(read, 1)
                    dve.wait_ge(read, n + 1)
                    pro(nc.vector.tensor_tensor(qk_c[:, which, :], rope_a[:], rope_b[:], ALU.add))

                first, second = r.steps()

                def slots(part):
                    def slot(i):
                        for name in part[i]:
                            step(name)
                    return slot

                if r.has_first and r.first_full:
                    attend(full, att_f, r.first, slots(first))
                    dve.wait_ge(full.normed, r.first * G + G)
                    if r.has_core:
                        dve.wait_ge(xz_done, r.core + 1)
                    nc.vector.tensor_tensor(x_mid[:], x_in[:], att_f[:].rearrange("p c h e -> p (c h e)"), ALU.add).then_inc(x_mid_a, 1)
                    dve.wait_ge(x_mid_a, r.first + 1)
                else:
                    for i in range(SLOTS):
                        slots(first)(i)
                if r.has_core:
                    attend(causal, att_c, r.core, slots(second))
                else:
                    for i in range(SLOTS):
                        slots(second)(i)

            nxt0 = chain_of(f_n.chain, CHAIN_NEXT_FULL, 0, begin=True)
            dve.wait_ge(x_loaded, 16)
            moments(nxt0, x_in, D, f_n.var)
            normalise_full(0)
            centre(nxt0, 0)
            split(full, f_buf, nxt0, 0, 0, qk_f)
            mask(full, f_buf, 0)
            rounds(dve, one)

        @block.tensor
        def _(pe):
            pe.wait_ge(loaded, ALL_LOADED)
            pe.wait_ge(consts_ready, 2)

            def mm(o, lhs_t, rhs, start=True, stop=True):
                return nc.tensor.matmul(o, lhs_t, rhs, start=start, stop=stop)

            def experts(k, m, wide):
                e, u = divmod(k, 3)
                ps = expert_bank(k, wide)
                if u < 2:
                    if k == 0:
                        pe.wait_ge(xm_tsb, m + 1)
                    if e and u == (1 if wide else 0):
                        pe.wait_ge(biased, m * E + e)
                    if wide and e and u == 0:
                        pe.wait_ge(relu, m * (2 * E) + 2 * e)
                    if u == 1 and not wide:
                        pe.wait_ge(relu, m * (2 * E) + 2 * e + 1)
                    for i in range(2):
                        j = 2 * u + i
                        last = mm(ps[:, i * T:(i + 1) * T], w_1[:, e, j * P:(j + 1) * P], xm_t[:])
                    last.then_inc(up, 1)
                else:
                    pe.wait_ge(relu, m * (2 * E) + 2 * e + 2)
                    for c in range(TC):
                        for j in range(J):
                            last = mm(ps[:, c * D:(c + 1) * D], hidden[:, e % 2, j, c * P:(c + 1) * P], w_2[:, e, j, :],
                                      start=j == 0, stop=j == J - 1)
                    last.then_inc(down, 1)

            def transpose2(dst, src, done):
                for c in range(TC):
                    last = nc.tensor.transpose(dst[:, c * P:(c + 1) * P], src(c), ident)
                last.then_inc(done, 1)

            def attend(core, buf, values, n, tr_free, wt_free, slot):
                _, q_stack, _, k_stack = buf

                def query_side(g, u):
                    c, i0, pairs, keys = core.q_units[u]
                    idx = g * core.nq + u
                    ps = SQ[idx % 2]
                    if idx >= 2:
                        pe.wait_ge(core.maxed, n * (G * core.nq) + idx - 1)
                    if core.causal:
                        mm(ps[:], ident_b[:], masks_b[:, QM0 if c == 0 else QM1, :], stop=False)
                    w = 2 * keys
                    for i in range(pairs):
                        pair = 2 * g + i0 + i
                        last = mm(ps[:, i * w:(i + 1) * w].rearrange("p (v k) -> p v k", k=keys),
                                  q_stack[0:ROWS, pair, c * P:(c + 1) * P], k_stack[0:ROWS, pair, :, 0:keys],
                                  start=not core.causal, stop=not core.causal or i == pairs - 1)
                    last.then_inc(core.scores_q, 1)

                def transpose_max(g):
                    pe.wait_ge(core.maxed, n * (G * core.nq) + (g + 1) * core.nq)
                    if g == 0 and tr_free:
                        pe.wait_ge(*tr_free)
                    if g >= 2:
                        pe.wait_ge(core.normed, n * G + g - 1)
                    for i in range(2):
                        for c in range(TC):
                            last = nc.tensor.transpose(tr_max[ROWS:ALL_ROWS, i * T + c * P:i * T + (c + 1) * P],
                                                       maxima[:, 2 * g + i, c, :], ident_b[:])
                    last.then_inc(core.max_t, 1)

                def key_side(g, u):
                    kc, i0, pairs, q0 = core.k_units[u]
                    idx = g * core.nk + u
                    ps = SK[idx % 2]
                    if u == 0:
                        pe.wait_ge(core.shift, n * G + g + 1)
                    if idx >= 2:
                        pe.wait_ge(core.probs, n * (G * core.nk) + idx - 1)
                    w = T - q0
                    if core.causal:
                        mm(ps[:], ident_b[:], masks_b[:, KM0 if kc == 0 else KM1, :], stop=False)
                    for i in range(2 * pairs):
                        pair, v = 2 * g + i0 + i // 2, i % 2
                        last = mm(ps[:, i * w:(i + 1) * w], k_stack[0:ALL_ROWS, pair, v, kc * P:(kc + 1) * P],
                                  q_stack[0:ALL_ROWS, pair, q0:T], start=not core.causal,
                                  stop=not core.causal or i == 2 * pairs - 1)
                    last.then_inc(core.scores_k, 1)

                def weigh(g):
                    pe.wait_ge(core.probs, n * (G * core.nk) + (g + 1) * core.nk)
                    if g:
                        pe.wait_ge(core.weighted_sb, n * G + g)
                    elif wt_free:
                        pe.wait_ge(*wt_free)
                    for kc in range(TC):
                        q0 = P if core.causal and kc else 0
                        for v in range(V):
                            last = mm(WT[v * QUAD:(v + 1) * QUAD, q0:T], values[:, kc, g * V + v, :],
                                      probs[:, g % 2, kc, v, q0:T], start=kc == 0, stop=kc == TC - 1)
                    last.then_inc(core.weighted, 1)

                def transpose_out(g):
                    pe.wait_ge(core.weighted_sb, n * G + g + 1)
                    pe.wait_ge(core.shift, n * G + min(g + 2, G))
                    if g:
                        pe.wait_ge(core.normed, n * G + g)
                    transpose2(TR, lambda c: wt_sb[:, g % 2, c * P:(c + 1) * P], core.out_t)

                pe.wait_ge(core.stacked_q, n * (16 * len(Q_TERMS)) + 16 * len(Q_TERMS))
                pe.wait_ge(core.masked, n + 1)
                query_side(0, 0)
                query_side(0, 1)
                slot(0)
                for u in range(2, core.nq):
                    query_side(0, u)
                for g in range(G):
                    more = g + 1 < G
                    if more:
                        query_side(g + 1, 0)
                    slot(3 * g + 1)
                    if more:
                        query_side(g + 1, 1)
                    transpose_max(g)
                    if g == 1:
                        pe.wait_ge(core.values, n + 1)
                    if g:
                        weigh(g - 1)
                    key_side(g, 0)
                    key_side(g, 1)
                    slot(3 * g + 2)
                    if more:
                        for u in range(2, core.nq):
                            query_side(g + 1, u)
                    if g:
                        transpose_out(g - 1)
                    for u in range(2, core.nk):
                        key_side(g, u)
                    slot(3 * g + 3)
                weigh(G - 1)
                slot(SLOTS - 1)
                transpose_out(G - 1)

            def transpose_full(b):
                pe.wait_ge(f_n.done, b + 1)
                transpose2(SIDE, lambda c: z_f[:, c, :], f_n.t)

            def one(r):
                n = r.core

                def step(name):
                    if name[1:].isdigit():
                        experts(int(name[1:]), r.experts, r.wide)
                    elif name == "zr_t":
                        pe.wait_ge(zr_done, n + 1)
                        transpose2(SIDE, lambda c: zr[:, c, :], c_n.t)
                    elif name == "lat":
                        pe.wait_ge(c_n.t_sb, n + 1)
                        for c in range(TC):
                            last = mm(SIDE[:, c * LAT:(c + 1) * LAT], z_t[:, c * P:(c + 1) * P], w_dkv[:])
                        last.then_inc(lat_ps, 1)
                    elif name == "q":
                        pe.wait_ge(lat_copied, n + 1)
                        mm(SIDE[:, 0:T], w_q[:], z_t[:])
                        mm(SIDE[:, T:2 * T], w_qr[:], z_t[:]).then_inc(q_ps, 1)
                    elif name == "lat_t":
                        pe.wait_ge(lat_done, n + 1)
                        pe.wait_ge(q_read, n + 1)
                        transpose2(SIDE, lambda c: lat_n[:, c, :], lat_tps)
                    elif name == "k":
                        pe.wait_ge(lat_tsb, n + 1)
                        mm(SIDE[:, 0:T], w_uk[:], lat_t[:])
                        mm(SIDE[:, T:2 * T], w_ukr[:], lat_t[:]).then_inc(k_ps, 1)
                    elif name == "v":
                        pe.wait_ge(k_read, n + 1)
                        for c in range(TC):
                            last = mm(SIDE[:, c * D:(c + 1) * D], lat_t[:, c * P:(c + 1) * P], w_uv[:])
                        last.then_inc(v_ps, 1)
                    elif name == "att_t":
                        pe.wait_ge(causal.normed, r.post * G + G)
                        if r.has_core:
                            pe.wait_ge(causal.values, n + 1)
                        transpose2(SIDE, lambda c: att_c[:, c, :, :].rearrange("p h e -> p (h e)"), att_tps)
                    elif name == "y":
                        pe.wait_ge(att_tsb, r.post + 1)
                        for c in range(TC):
                            last = mm(SIDE[:, c * D:(c + 1) * D], att_t[:, c * P:(c + 1) * P], w_o[:])
                        last.then_inc(y_ps, 1)
                    elif name == "xm_t":
                        pe.wait_ge(xm_done, r.post + 1)
                        if r.has_next and r.next_full:
                            pe.wait_ge(centred, r.next + 1)
                        transpose2(SIDE, lambda c: xm[:, c, :], xm_tps)
                    elif name == "logit":
                        pe.wait_ge(xm_tsb, r.post + 1)
                        for c in range(TC):
                            last = mm(SIDE[:, c * E:(c + 1) * E], xm_t[:, c * P:(c + 1) * P], w_gate[:])
                        last.then_inc(logit_ps, 1)
                    elif name == "f_t":
                        if r.has_post:
                            pe.wait_ge(acc_ready, r.post + 1)
                        transpose_full(r.next)
                    elif name == "b_t":
                        pe.wait_ge(b_n.done, r.first + 1)
                        transpose2(SQ[0], lambda c: z_f[:, c, :], b_n.t)
                    elif name == "b_w":
                        pe.wait_ge(b_n.t_sb, r.first + 1)
                        mm(SQ[1][:, 0:T], w_b[:], z_bt[:]).then_inc(t_ps, 1)
                    elif name == "b_s":
                        pe.wait_ge(t_sb, r.first + 1)
                        for c in range(TC):
                            last = mm(SK[0][:, c * T:(c + 1) * T], t_t[:, c * P:(c + 1) * P], z_bt[:])
                        last.then_inc(s_ps, 1)
                    elif name == "b_pt":
                        pe.wait_ge(p_done, r.first + 1)
                        for kc in range(TC):
                            for c in range(TC):
                                last = nc.tensor.transpose(SK[1][:, kc * T + c * P:kc * T + (c + 1) * P],
                                                           p_band[:, c, kc * P:(kc + 1) * P], ident)
                        last.then_inc(pt_ps, 1)
                    elif name == "b_ra":
                        pe.wait_ge(pt_sb, r.first + 1)
                        for c in range(TC):
                            for kc in range(TC):
                                last = mm(SQ[0][:, c * D:(c + 1) * D], pt_band[:, kc, c * P:(c + 1) * P], z_f[:, kc, :],
                                          start=kc == 0, stop=kc == TC - 1)
                        last.then_inc(ra_ps, 1)

                first, second = r.steps()

                def slots(part):
                    def slot(i):
                        for name in part[i]:
                            step(name)
                    return slot

                if r.has_first and r.first_full:
                    tr_free = (causal.normed, (r.s - 1) * G) if r.like >= 2 else None
                    attend(full, f_buf, values_f, r.first, tr_free, None, slots(first))
                else:
                    for i in range(SLOTS):
                        slots(first)(i)
                if r.has_core:
                    if r.has_first and r.first_full:
                        tr_free = (full.normed, (r.first + 1) * G)
                    else:
                        tr_free = (causal.normed, (r.s - 1) * G) if r.like >= 2 else None
                    wt_free = (biased, (r.experts + 1) * E) if r.wide and r.has_experts else None
                    attend(causal, c_buf, values_c, n, tr_free, wt_free, slots(second))
                else:
                    for i in range(SLOTS):
                        slots(second)(i)

            transpose_full(0)
            rounds(pe, one)


def constants():
    import numpy as np

    c = np.zeros((P, CST_COLS), np.float32)

    def put(name, a):
        c[:, CST[name][0]:CST[name][1]] = a

    r = np.arange(P)
    put("ident", np.eye(P, dtype=np.float32))
    later_key = np.where(r[None, :] > r[:, None], np.float32(-BIG), np.float32(0))
    zero = np.zeros((P, P), np.float32)
    put("qmask0", np.tile(later_key, (1, V)))
    put("qmask1", np.tile(np.concatenate([zero, later_key], 1), (1, 2)))
    put("kmask0", np.tile(np.concatenate([later_key.T, zero], 1), (1, 2)))
    put("kmask1", np.tile(later_key.T, (1, V)))
    k = np.arange(T)
    put("band", np.concatenate([np.where(np.abs(c0 * P + r[:, None] - k[None, :]) > BAND, np.float32(-BIG), np.float32(0))
                                for c0 in range(TC)], 1))
    half = HD // 2
    inv = (1.0 / np.float32(10000.0) ** (np.arange(half, dtype=np.float32) / np.float32(half))).astype(np.float32)
    ang = np.arange(T, dtype=np.float32)[:, None] * inv[None, :]
    dim = (r // NP) % HD
    cos, sin = np.cos(ang).T[dim % half], np.sin(ang).T[dim % half] * np.where(dim < half, -1, 1)[:, None]
    scale = 1.0 / np.sqrt(HD)
    put("cos_q", cos * scale)
    put("sin_q", sin * scale)
    put("cos_k", cos)
    put("sin_k", sin)
    put("headmask", (r % TERM)[:, None] // HD == np.arange(2)[None, :])
    put("shiftsel", -((r - ROWS)[:, None] == np.arange(2)[None, :]).astype(np.float32))
    put("priority", np.arange(E, 0, -1)[None, :])
    return c


def kernel(**inputs):
    import numpy as np
    import concourse.bacc as bacc
    from concourse.bass_utils import run_bass_kernel_spmd

    a = {k.replace("L0_", ""): np.asarray(v) for k, v in inputs.items()}
    order = np.arange(D).reshape(NP, TERM).T.reshape(-1)
    partner = (order // HD) * HD + (order % HD + HD // 2) % HD
    pad = np.zeros(D - LAT, np.float32)
    arrays = {
        "x": a["attn_a_x"], "wb": a["attn_b_W"],
        "wq": a["ffn_Wq"].T[:, order], "wqr": a["ffn_Wq"].T[:, partner],
        "wdkv": a["ffn_Wdkv"].T,
        "wuk": a["ffn_Wuk"].T[:, order], "wukr": a["ffn_Wuk"].T[:, partner], "wuv": a["ffn_Wuv"].T,
        "wo": a["ffn_Wo"].T, "gate": a["ffn_gate_w"].T,
        "w1": a["ffn_W1"].transpose(2, 0, 1),
        "w2": a["ffn_W2"].reshape(E, D, J, P).transpose(3, 0, 2, 1),
        "b1": a["ffn_b1"].reshape(E * J, P).T,
        "b2": np.broadcast_to(a["ffn_b2"][None], (P, E, D)),
        "gate_b": np.broadcast_to(a["ffn_gate_b"][None], (P, E)),
        "cols": np.stack([a["ffn_norm1_w"], a["ffn_norm2_w"], np.concatenate([a["ffn_ln_g"], pad]),
                          np.concatenate([a["ffn_ln_b"], pad])], 1),
        "cst": constants(),
    }
    arrays = {k: np.ascontiguousarray(v) for k, v in arrays.items()}
    nc = bacc.Bacc("TRN2", target_bir_lowering=False, num_devices=1)
    args = [nc.dram_tensor(f"in_{k}", v.shape, mybir.dt.from_np(v.dtype), kind="ExternalInput").ap()
            for k, v in arrays.items()]
    out = nc.dram_tensor("out_x", (B, T, D), F32, kind="ExternalOutput").ap()
    build(nc, *args, out)
    r = run_bass_kernel_spmd(nc, [{f"in_{k}": v for k, v in arrays.items()}], core_ids=[0])
    return r.results[0]["out_x"]
```

```python
from contextlib import ExitStack

import concourse.bass as bass
from concourse import mybir

F32 = mybir.dt.float32
BF16 = mybir.dt.bfloat16
ALU = mybir.AluOpType
ACT = mybir.ActivationFunctionType
AX = mybir.AxisListType.X

B, T, D = 32, 256, 128
P = 128
TC = T // P
H, HD = 16, 8
G, V = 4, 4
NP = H // 2
QUAD = 32
TERM = 2 * HD
Q_TERMS, K_TERMS = "hhmmlh", "hmhmhl"
ROWS = len(Q_TERMS) * TERM
ALL_ROWS = ROWS + 2
LAT = 64
E, HID = 4, 512
J = HID // P
BAND = 64
LN_EPS, RMS_EPS = 1e-5, 1e-6
BIG = 1e30

CST, CST_COLS = {}, 0
for _name, _n in (("ident", P), ("headmask", 2), ("shiftsel", 2), ("priority", E),
                  ("qmask0", V * P), ("qmask1", 2 * T), ("kmask0", 2 * T), ("kmask1", V * P),
                  ("band", TC * T), ("cos_q", T), ("sin_q", T), ("cos_k", T), ("sin_k", T)):
    CST[_name] = (CST_COLS, CST_COLS + _n)
    CST_COLS += _n
FIRST_CONSTS = CST["priority"][1]
QM0, QM1, KM0, KM1 = range(4)

SLOTS = 4 * G + 2
ROUND_A = {
    "pe": (
        "u2 out zr_t | lat | d0 u3 | q u4 | - | lat_t | k d1 | v | u5 | - | - | u6 | - | d2 | - | - | u7 | -",
        "f_t f_out | d3 | - | att_t | - | y | - | - | - | xm_t | - | - | n0 | - | logit | - | n1 | -"),
    "dve": (
        "out | lat | - | c0 q | - | split_q | k c1 | - | split_k | - | - | - | - | - | - | f_norm_a c2 | - | "
        "f_norm_b mask",
        "f_out | f_centre | c3 | - | - | y | - | f_split xm | - | - | - | norm_a | - | - | norm_b norm_c | "
        "route_a route_b | - | f_mask"),
    "act": (
        "r2 zr_t lat | - | r3 | - | - | lat_t r4 | - | v | - | r5 | - | r6 | - | - | - | - | - | -",
        "- | r7 | - | att_t | - | - | save_x | f_split save | - | xm_t | - | - | - | rn0 | - | - | rn1 | -"),
    "pool": (
        "- | - | - | - | - | - | - | - | lat | - | - | - | - | - | - | f_norm_a | - | -",
        "- | - | - | - | - | - | - | - | - | - | y_rms norm_a norm_b | - | - | - | - | - | - | -"),
    "sp": (
        "- | - | - | - | - | - | split_q | - | - | - | - | - | - | split_k | - | - | - | -",
        "x_load | keep | - | - | - | - | - | f_split | - | - | - | - | - | - | - | - | - | -"),
}
ROUND_B = {
    "pe": (
        "b_t zr_t out u2 b_w lat | - | b_s | u3 | q d0 u4 lat_t | d1 | k b_pt b_ra | v | u5 u6 d2 | - | u7 | "
        "- | - | - | - | - | - | -",
        "d3 | att_t | y | - | - | - | - | - | xm_t | - | - | - | n0 | - | logit | - | n1 | -"),
    "dve": (
        "b_t out | - | lat b_s | - | q c0 split_q | c1 | k split_k | - | b_ra | mask | f_norm_a | - | - | - "
        "| c2 | - | - | b_end",
        "f_norm_b | c3 | y | - | xm | - | - | norm_a | - | - | - | - | route_a norm_b norm_c | - | - | - | "
        "route_b | -"),
    "act": (
        "b_t zr_t | b_w r2 | lat | r3 | b_soft | r4 lat_t b_pt | v | - | r5 r6 r7 | - | - | - | - | - | - | "
        "- | - | -",
        "att_t | - | - | - | - | - | - | save_x | xm_t | - | - | save | - | rn0 | - | - | rn1 | -"),
    "pool": (
        "- | - | - | - | - | - | - | - | lat | - | - | - | - | - | - | - | - | -",
        "- | - | - | f_norm_a y_rms | norm_a | - | - | norm_b | - | - | - | - | - | - | - | - | - | -"),
    "sp": (
        "- | - | - | - | - | split_q split_k | - | - | - | - | - | - | - | - | x_load | keep | - | -",
        "- | - | - | - | - | - | - | - | - | - | - | - | - | - | - | - | - | -"),
}
NORM = ("norm_a", "norm_b", "norm_c")
PRO = ("save", "zr_t", "lat", "q", "split_q", "lat_t", "k", "v", "split_k", "mask")
POST = ("out", "att_t", "y", "y_rms", "xm", "xm_t", "logit", "route_a", "route_b")
NEXT = ("x_load", "save_x", "f_norm_a", "f_norm_b", "f_t", "f_centre", "f_split", "f_mask")


class Round:

    def __init__(self, s, like):
        self.s, self.like = s, like
        self.has_first, self.has_next = like < 2 * B, like + 1 < 2 * B
        self.has_core, self.has_post, self.has_experts = (d <= like < 2 * B + d for d in (1, 2, 3))
        self.first_full, self.next_full = like < B, like + 1 < B
        self.wide = self.has_first and not self.first_full
        self.first = s if self.first_full else s - B
        self.next = s + 1 if self.next_full else s + (1 - B)
        self.core, self.post, self.experts = s - 1, s - 2, s - 3

    def steps(self, engine):
        def kept(name):
            if name[0] in "urdc" and name[1:].isdigit() or name == "keep":
                return self.has_experts
            if name[-1].isdigit():
                return self.has_post
            if name in PRO:
                return self.has_core
            if name in POST:
                return self.has_post
            if name in NORM:
                return self.has_first
            if name in ("f_t", "f_centre", "f_split", "f_mask"):
                return self.next_full
            if name in NEXT:
                return self.has_next
            if name == "f_out":
                return self.has_first and self.first_full
            return self.has_first and not self.first_full

        parts = (ROUND_B if self.wide else ROUND_A)[engine]
        return [[[n for n in slot.split() if n != "-" and kept(n)] for slot in part.split("|")] for part in parts]


def rounds(engine, one):
    for lo, hi in ((0, 4), (4, B - 1), (B - 1, B + 3), (B + 3, 2 * B - 1), (2 * B - 1, 2 * B + 3)):
        if hi - lo > 4:
            with engine.Fori(lo, hi, 1) as s:
                one(Round(s, lo))
        else:
            for s in range(lo, hi):
                one(Round(s, s))


class Core:

    def __init__(self, kind, sem):
        self.kind, self.causal = kind, kind == "causal"
        if self.causal:
            self.q_units = [(0, 0, 2, P), (1, 0, 1, T), (1, 1, 1, T)]
            self.k_units = [(0, 0, 1, 0), (0, 1, 1, 0), (1, 0, 2, P)]
        else:
            self.q_units = [(c, i, 1, T) for c in range(TC) for i in (0, 1)]
            self.k_units = [(c, i, 1, 0) for c in range(TC) for i in (0, 1)]
        self.nq, self.nk = len(self.q_units), len(self.k_units)
        self.parts = 1 if kind == "full" else 2
        self.high, self.mid, self.low = (sem(f"{kind}_{n}_part") for n in ("high", "mid", "low"))
        self.stacked_q = sem(f"{kind}_q_stacked")
        self.stacked_k = sem(f"{kind}_k_stacked")
        self.masked = sem(f"{kind}_k_masked")
        self.values = sem(f"{kind}_values_ready")
        self.scores_q = sem(f"{kind}_scores_q")
        self.maxed = sem(f"{kind}_maxed")
        self.max_t = sem(f"{kind}_max_transposed")
        self.shift = sem(f"{kind}_shift_ready")
        self.scores_k = sem(f"{kind}_scores_k")
        self.probs = sem(f"{kind}_probs_ready")
        self.weighted = sem(f"{kind}_weighted")
        self.weighted_sb = sem(f"{kind}_weighted_sb")
        self.out_t = sem(f"{kind}_out_transposed")
        self.recip = sem(f"{kind}_denominators")
        self.normed = sem(f"{kind}_normed")


class Norm:

    def __init__(self, kind, sem):
        self.chain = sem(f"{kind}_dve_chain")
        self.var, self.rstd = sem(f"{kind}_var"), sem(f"{kind}_rstd")
        self.done = sem(f"{kind}_normalised")
        self.t, self.t_sb = sem(f"{kind}_norm_t"), sem(f"{kind}_norm_t_sb")


CHAIN_NEXT_FULL, CHAIN_NEXT_BAND, CHAIN_BAND, CHAIN_NORM, CHAIN_PRO, CHAIN_POST = 5, 2, 4, 4, 6, 7


def build(nc, x, wb, wq, wqr, wdkv, wuk, wukr, wuv, wo, gate, w1, w2, b1, b2, gate_b, cols, cst, out):
    with ExitStack() as ctx:
        def sb(name, shape, dt=F32):
            return ctx.enter_context(nc.sbuf_tensor(name, shape, dt))

        def sem(name):
            return ctx.enter_context(nc.semaphore(name))

        w_b = sb("w_b", [P, D])
        w_q, w_qr = sb("w_q", [P, D]), sb("w_qr", [P, D])
        w_dkv = sb("w_dkv", [P, LAT])
        w_uk, w_ukr, w_uv = sb("w_uk", [LAT, D]), sb("w_ukr", [LAT, D]), sb("w_uv", [LAT, D])
        w_o = sb("w_o", [P, D])
        w_gate = sb("w_gate", [P, E])
        w_1 = sb("w_1", [P, E, HID])
        w_2 = sb("w_2", [P, E, J, D])
        b_1 = sb("b_1", [P, E * J])
        b_2 = sb("b_2", [P, E, D])
        b_gate = sb("b_gate", [P, E])
        col = sb("col", [P, 4])
        c_sb = sb("c_sb", [P, CST_COLS])
        ident_b = sb("ident_b", [P, P], BF16)
        masks_b = sb("masks_b", [P, 4, 512], BF16)
        minus_half = sb("minus_half", [P, TC])

        def const(name):
            a, b = CST[name]
            return c_sb[:, a:b]

        ident = const("ident")

        x_all = sb("x_all", [P, B * T])
        x_in = sb("x_in", [P, T])
        x_res = sb("x_res", [P, T])
        x_mid = sb("x_mid", [P, T])
        z_f = sb("z_f", [P, TC, D])
        z = sb("z", [P, TC, D])
        xz_c = sb("xz_c", [P, T])
        z_old, xz_old = sb("z_old", [P, T]), sb("xz_old", [P, T])
        zr = sb("zr", [P, TC, D])
        z_t = sb("z_t", [P, T])
        stats = sb("stats", [P, TC, 6])
        mv = sb("mv", [P, TC, 2])
        var_eps, rstd = sb("var_eps", [P, TC]), sb("rstd", [P, TC])
        sqr = sb("sqr", [P, TC])
        ms, rrms = sb("ms", [P, TC]), sb("rrms", [P, TC])
        lat_sb = sb("lat_sb", [P, TC * LAT])
        lat_n = sb("lat_n", [P, TC, P])
        lat_t = sb("lat_t", [LAT, T])
        rope_a, rope_b = sb("rope_a", [P, T]), sb("rope_b", [P, T])
        mean = sb("mean", [P, 2])
        spacer = sb("spacer", [P, 1])
        qk_f = sb("qk_f", [P, 1, T])
        qk_c = sb("qk_c", [P, 2, T])
        rest = sb("rest", [P, 2, T])

        def stack_buffers(kind, n):
            parts = {x: sb(f"part_{x}_{kind}", [P, n, T], BF16) for x in "hml"}
            return (parts, sb(f"q_stack_{kind}", [P, NP, T], BF16), sb(f"k_raw_{kind}", [ROWS, NP, T], BF16),
                    sb(f"k_stack_{kind}", [P, NP, 2, T], BF16))

        f_buf, c_buf = stack_buffers("full", 1), stack_buffers("causal", 2)
        maxima = sb("maxima", [P, NP, TC, 2], BF16)
        probs = sb("probs", [P, 2, TC, V, T])
        values_f, values_c = sb("values_f", [P, TC, H, QUAD]), sb("values_c", [P, TC, H, QUAD])
        wt_sb = sb("wt_sb", [P, 2, T])
        rsum = sb("rsum", [P, G, TC, V])
        att_f, att_c = sb("att_f", [P, TC, H, HD]), sb("att_c", [P, TC, H, HD])
        att_t = sb("att_t", [P, T])
        y1 = sb("y1", [P, TC, D])
        sq = sb("sq", [P, TC, D])
        xm = sb("xm", [P, TC, D])
        xm_t = sb("xm_t", [P, T])
        logits = sb("logits", [P, TC, E])
        lmax, rmax = sb("lmax", [P, TC]), sb("rmax", [P, TC])
        ranked = sb("ranked", [P, TC, E])
        onehot = sb("onehot", [P, TC, E])
        hidden = sb("hidden", [P, 2, J, T])
        y_b = sb("y_b", [P, TC, D])
        acc = sb("acc", [P, T])
        acc_out = sb("acc_out", [P, T])
        t_t = sb("t_t", [P, T])
        s_band = sb("s_band", [P, TC, T])
        p_band, pt_band = sb("p_band", [P, TC, T]), sb("pt_band", [P, TC, T])
        bmax, nmax = sb("bmax", [P, TC]), sb("nmax", [P, TC])
        sum_band, r_band = sb("sum_band", [P, TC]), sb("r_band", [P, TC])
        z_bt = sb("z_bt", [P, T])
        xz, ra = sb("xz", [P, T]), sb("ra", [P, TC, D])

        bank = [ctx.enter_context(nc.psum_tensor(f"bank{i}", [P, 512], F32)) for i in range(8)]
        SQ, SK, WT, TR, SIDE, EX = bank[0:2], bank[2:4], bank[4], bank[5], bank[6], bank[7]
        tr_max = TR[:, 256:512].bitcast(BF16)

        consts_loaded, masks_ready = sem("consts_loaded"), sem("causal_masks_ready")
        loaded, consts_ready, zeroed, ones_set = sem("weights_loaded"), sem("consts_ready"), sem("zeroed"), sem("ones_set")
        x_loaded, x_moved = sem("x_loaded"), sem("x_moved")
        full, causal = Core("full", sem), Core("causal", sem)
        f_n, c_n, b_n = Norm("full", sem), Norm("causal", sem), Norm("band", sem)
        norm_chain = sem("norm_dve_chain")
        post_chain, band_chain = sem("post_dve_chain"), sem("banded_dve_chain")
        x_mid_a, x_mid_b = sem("x_mid_full"), sem("x_mid_banded")
        centred = sem("centred")
        res_done = sem("x_res_ready")
        saved, xz_done, lat_copied, q_read, k_read = (sem(n) for n in (
            "z_saved", "x_plus_z", "latent_copied", "q_read", "k_read"))
        acc_ready, routed, zr_done, y1_done = sem("acc_ready"), sem("routed"), sem("zr_ready"), sem("y1_ready")
        c_ms, c_rrms = sem("z_mean_square"), sem("z_inverse_rms")
        lat_ps, lat_var, lat_rstd = sem("latent_psum"), sem("latent_var"), sem("latent_rstd")
        lat_done, lat_tps, lat_tsb = sem("latent_normalised"), sem("latent_t_psum"), sem("latent_t_sb")
        q_ps, k_ps, v_ps = sem("q_psum"), sem("k_psum"), sem("v_psum")
        att_tps, att_tsb, y_ps = sem("att_t_psum"), sem("att_t_sb"), sem("att_projected")
        y_ms, y_rrms = sem("y_mean_square"), sem("y_inverse_rms")
        xm_done, xm_tps, xm_tsb, logit_ps = sem("xm_ready"), sem("xm_t_psum"), sem("xm_t_sb"), sem("logits_psum")
        t_ps, t_sb, s_ps, bmax_done = sem("band_t_psum"), sem("band_t_sb"), sem("band_scores"), sem("band_max")
        p_done, pt_ps, pt_sb, ra_ps = sem("band_probs"), sem("band_pt_psum"), sem("band_pt_sb"), sem("band_weighted")
        up, relu, down = sem("expert_up"), sem("expert_relu"), sem("expert_down")
        biased, combined = sem("expert_biased"), sem("expert_combined")
        left = sem("acc_out_left")

        x_d = x.rearrange("b (c p) d -> b p c d", p=P)
        out_d = out.rearrange("b (c p) d -> b p c d", p=P)

        LOADS = [(w_b[:], wb), (w_q[:], wq), (w_qr[:], wqr), (w_dkv[:], wdkv), (w_uk[:], wuk), (w_ukr[:], wukr),
                 (w_uv[:], wuv), (w_o[:], wo), (w_gate[:], gate), (w_1[:], w1), (w_2[:], w2), (b_1[:], b1),
                 (b_2[:], b2), (b_gate[:], gate_b), (col[:], cols), (c_sb[:, FIRST_CONSTS:], cst[:, FIRST_CONSTS:])]
        ALL_LOADED = 16 * len(LOADS)

        def up_bank(k, wide):
            return TR if wide and k % 2 and k > 2 else EX

        def down_bank(e, wide):
            return WT if wide and e < E - 1 else EX

        def expert_of(name):
            kind = name.rstrip("0123456789")
            return (kind, int(name[len(kind):])) if kind != name else ("", 0)

        block = ctx.enter_context(nc.Block())

        @block.sync
        def _(sp):
            def stack(core, buf, n, which, sides):
                parts, q_stack, k_raw, _ = buf
                count = n * core.parts + which + 1
                for part, ready in (("h", core.high), ("m", core.mid), ("l", core.low)):
                    sp.wait_ge(ready, count)
                    for terms, dst, done, side in ((Q_TERMS, q_stack, core.stacked_q, "q"), (K_TERMS, k_raw, core.stacked_k, "k")):
                        for t, of in enumerate(terms):
                            if of == part and side in sides:
                                sp.dma_start(dst[t * TERM:(t + 1) * TERM, :, :].rearrange("r g t -> r (g t)"),
                                             parts[part][:, which, :]).then_inc(done, 16)

            def one(r):
                def step(name):
                    if name == "split_q":
                        stack(causal, c_buf, r.core, 0, "q")
                    elif name == "split_k":
                        stack(causal, c_buf, r.core, 1, "k")
                    elif name == "f_split":
                        stack(full, f_buf, r.next, 0, "qk")
                    elif name == "x_load":
                        sp.wait_ge(res_done, r.s + 1)
                        if r.next_full:
                            load_x(r.next)
                        else:
                            sp.wait_ge(left, 16 * (B - 4) if r.like < B + 3 else 16 * B)
                            sp.dma_start(x_in[:], x_all[:, bass.ds(r.next * T, T)]).then_inc(x_moved, 16)
                    elif name == "keep":
                        sp.wait_ge(combined, r.experts * E + E)
                        if r.like - 3 < B:
                            sp.dma_start(x_all[:, bass.ds(r.experts * T, T)], acc_out[:]).then_inc(left, 16)
                        else:
                            sp.dma_start(out_d[bass.ds(r.experts - B, 1), :, :, :].rearrange("o p c d -> (o p) c d"),
                                         acc_out[:].rearrange("p (c d) -> p c d", c=TC)).then_inc(left, 16)

                for part in r.steps("sp"):
                    for slot in part:
                        for name in slot:
                            step(name)

            def load_x(b):
                sp.dma_start(x_in[:].rearrange("p (c d) -> p c d", c=TC),
                             x_d[bass.ds(b, 1), :, :, :].rearrange("o p c d -> (o p) c d")).then_inc(x_loaded, 16)

            load_x(0)
            sp.dma_start(c_sb[:, 0:FIRST_CONSTS], cst[:, 0:FIRST_CONSTS]).then_inc(consts_loaded, 16)
            stack(full, f_buf, 0, 0, "qk")
            for dst, src in LOADS:
                sp.dma_start(dst, src).then_inc(loaded, 16)
            rounds(sp, one)
            sp.wait_ge(left, 16 * 2 * B)

        @block.gpsimd
        def _(pool):
            for tensor, value in ((values_f, 0.0), (values_c, 0.0), (lat_n, 0.0), (minus_half, -0.5)):
                nc.gpsimd.memset(tensor[:], value).then_inc(zeroed, 1)
            pool.wait_ge(zeroed, 4)
            for tensor in (values_f, values_c):
                nc.gpsimd.memset(tensor[:, :, :, HD:HD + 1], 1.0).then_inc(ones_set, 1)
            pool.wait_ge(ones_set, 2)

            def inverse_root(dst, src, ready, done, n):
                pool.wait_ge(ready, n + 1)
                nc.gpsimd.tensor_tensor(dst[:], src[:], minus_half[:], ALU.pow).then_inc(done, 1)

            def one(r):
                def step(name):
                    if name == "norm_a":
                        inverse_root(rstd, var_eps, c_n.var, c_n.rstd, r.s)
                    elif name == "norm_b":
                        inverse_root(rrms, ms, c_ms, c_rrms, r.s)
                        pool.wait_ge(c_n.done, r.s + 1)
                        nc.gpsimd.tensor_tensor(xz_c[:], x_mid[:], z[:].rearrange("p c d -> p (c d)"), ALU.add).then_inc(xz_done, 1)
                    elif name == "lat":
                        inverse_root(rstd, var_eps, lat_var, lat_rstd, r.core)
                    elif name == "y_rms":
                        inverse_root(rrms, ms, y_ms, y_rrms, r.post)
                    elif name == "f_norm_a":
                        which = f_n if r.next_full else b_n
                        inverse_root(rstd, var_eps, which.var, which.rstd, r.next)

                for part in r.steps("pool"):
                    for slot in part:
                        for name in slot:
                            step(name)

            inverse_root(rstd, var_eps, f_n.var, f_n.rstd, 0)
            rounds(pool, one)

        @block.scalar
        def _(act):
            act.wait_ge(ones_set, 2)

            def activate(k, m, wide):
                e, u = divmod(k, 2)
                ps = up_bank(k, wide)
                act.wait_ge(up, m * (2 * E) + k + 1)
                if e >= 2 and u == 0:
                    act.wait_ge(down, m * E + e - 1)
                for i in range(2):
                    j = 2 * u + i
                    last = nc.scalar.activation(hidden[:, e % 2, j, :], ps[:, i * T:(i + 1) * T], ACT.Relu,
                                                bias=b_1[:, e * J + j:e * J + j + 1])
                last.then_inc(relu, 1)

            def copy_x(r, normed, b):
                act.wait_ge(normed, b + 1)
                if r is not None and r.has_first:
                    act.wait_ge(x_mid_a if r.first_full else x_mid_b, r.first + 1)
                nc.scalar.copy(x_res[:], x_in[:]).then_inc(res_done, 1)

            def copy_values_full(b):
                act.wait_ge(f_n.done, b + 1)
                for c in range(TC):
                    last = nc.scalar.copy(values_f[:, c, :, 0:HD].rearrange("p (g f) e -> p g f e", g=NP),
                                          z_f[:, c, :].rearrange("p (f e g) -> p g f e", f=2, e=HD))
                last.then_inc(full.values, 1)

            def attend(core, buf, n, slot):
                q_stack = buf[1]

                def copy_weighted(g):
                    act.wait_ge(core.weighted, n * G + g + 1)
                    nc.scalar.copy(wt_sb[:, g % 2, :], WT[:, 0:T]).then_inc(core.weighted_sb, 1)

                def exponentials(g, u):
                    kc, i0, pairs, q0 = core.k_units[u]
                    idx = g * core.nk + u
                    act.wait_ge(core.scores_k, n * (G * core.nk) + idx + 1)
                    if u == 0 and g >= 2:
                        act.wait_ge(core.weighted, n * G + g - 1)
                    w = T - q0
                    nc.scalar.activation(probs[:, g % 2, kc, 2 * i0:2 * (i0 + pairs), q0:T],
                                         SK[idx % 2][:, 0:2 * pairs * w].rearrange("p (v q) -> p v q", q=w),
                                         ACT.Exp).then_inc(core.probs, 1)

                slot(0)
                for g in range(G):
                    slot(4 * g + 1)
                    act.wait_ge(core.max_t, n * G + g + 1)
                    nc.scalar.copy(q_stack[ROWS:ALL_ROWS, 2 * g:2 * g + 2, :],
                                   tr_max[ROWS:ALL_ROWS, :].rearrange("p (i q) -> p i q", i=2)).then_inc(core.shift, 1)
                    if g:
                        copy_weighted(g - 1)
                    slot(4 * g + 2)
                    exponentials(g, 0)
                    exponentials(g, 1)
                    slot(4 * g + 3)
                    for u in range(2, core.nk):
                        exponentials(g, u)
                    slot(4 * g + 4)
                copy_weighted(G - 1)
                slot(SLOTS - 1)

            def one(r):
                if r.like == 1:
                    act.wait_ge(loaded, ALL_LOADED)

                def step(name):
                    kind, k = expert_of(name)
                    if kind == "r":
                        activate(k, r.experts, r.wide)
                    elif kind == "rn":
                        activate(k, r.post, False)
                    elif name == "save":
                        act.wait_ge(xz_done, r.core + 1)
                        if r.has_post:
                            act.wait_ge(acc_ready, r.post + 1)
                        nc.scalar.copy(z_old[:], z[:].rearrange("p c d -> p (c d)"))
                        nc.scalar.copy(xz_old[:], xz_c[:]).then_inc(saved, 1)
                    elif name == "zr_t":
                        act.wait_ge(c_n.t, r.core + 1)
                        nc.scalar.activation(z_t[:], SIDE[:, 0:T], ACT.Copy, scale=col[:, 0:1]).then_inc(c_n.t_sb, 1)
                    elif name == "lat":
                        act.wait_ge(lat_ps, r.core + 1)
                        nc.scalar.copy(lat_sb[:], SIDE[:, 0:TC * LAT]).then_inc(lat_copied, 1)
                    elif name == "lat_t":
                        act.wait_ge(lat_tps, r.core + 1)
                        nc.scalar.activation(lat_t[:], SIDE[0:LAT, 0:T], ACT.Identity, scale=col[0:LAT, 2:3],
                                             bias=col[0:LAT, 3:4]).then_inc(lat_tsb, 1)
                    elif name == "v":
                        act.wait_ge(v_ps, r.core + 1)
                        for c in range(TC):
                            last = nc.scalar.copy(values_c[:, c, :, 0:HD],
                                                  SIDE[:, c * D:(c + 1) * D].rearrange("p (h e) -> p h e", e=HD))
                        last.then_inc(causal.values, 1)
                    elif name == "att_t":
                        act.wait_ge(att_tps, r.post + 1)
                        nc.scalar.copy(att_t[:], SIDE[:, 0:T]).then_inc(att_tsb, 1)
                    elif name == "xm_t":
                        act.wait_ge(xm_tps, r.post + 1)
                        if r.has_experts:
                            act.wait_ge(up, (r.experts + 1) * (2 * E))
                        nc.scalar.activation(xm_t[:], SIDE[:, 0:T], ACT.Copy, scale=col[:, 1:2]).then_inc(xm_tsb, 1)
                    elif name == "f_split":
                        copy_values_full(r.next)
                    elif name == "save_x":
                        copy_x(r, f_n.done if r.next_full else b_n.done, r.next)
                    elif name == "b_t":
                        act.wait_ge(b_n.t, r.first + 1)
                        nc.scalar.copy(z_bt[:], SQ[0][:, 0:T]).then_inc(b_n.t_sb, 1)
                    elif name == "b_w":
                        act.wait_ge(t_ps, r.first + 1)
                        nc.scalar.copy(t_t[:], SQ[1][:, 0:T]).then_inc(t_sb, 1)
                    elif name == "b_soft":
                        act.wait_ge(bmax_done, r.first + 1)
                        for c in range(TC):
                            last = nc.scalar.activation(p_band[:, c, :], s_band[:, c, :], ACT.Exp, bias=nmax[:, c:c + 1],
                                                        accum_out=sum_band[:, c:c + 1])
                        last.then_inc(p_done, 1)
                    elif name == "b_pt":
                        act.wait_ge(pt_ps, r.first + 1)
                        nc.scalar.copy(pt_band[:].rearrange("p c q -> p (c q)"), SK[1][:, 0:TC * T]).then_inc(pt_sb, 1)

                first, second = r.steps("act")

                def slots(part):
                    def slot(i):
                        for name in part[i]:
                            step(name)
                    return slot

                if r.has_first and r.first_full:
                    attend(full, f_buf, r.first, slots(first))
                else:
                    for i in range(SLOTS):
                        slots(first)(i)
                if r.has_core:
                    attend(causal, c_buf, r.core, slots(second))
                else:
                    for i in range(SLOTS):
                        slots(second)(i)

            copy_x(None, f_n.done, 0)
            copy_values_full(0)
            rounds(act, one)

        @block.vector
        def _(dve):
            dve.wait_ge(consts_loaded, 16)
            dve.wait_ge(ones_set, 2)
            nc.vector.tensor_copy(ident_b[:], ident)
            for _, _, _, k_stack in (f_buf, c_buf):
                last = nc.vector.memset(k_stack[ROWS:ALL_ROWS, :, :, :], 1.0)
            last.then_inc(consts_ready, 1)
            dve.wait_ge(consts_ready, 1)
            for _, _, _, k_stack in (f_buf, c_buf):
                for v in range(2):
                    last = nc.vector.tensor_scalar(k_stack[ROWS:ALL_ROWS, :, v, :], k_stack[ROWS:ALL_ROWS, :, v, :],
                                                   const("shiftsel")[ROWS:ALL_ROWS, v:v + 1], None, ALU.mult)
            last.then_inc(consts_ready, 1)

            done = {}

            def chain_of(chain, per, n, begin=False):
                key = chain.name
                if begin:
                    done[key] = 0

                def link(ins):
                    done[key] += 1
                    assert done[key] <= per, (key, per)
                    ins.then_inc(chain, 1)
                    dve.wait_ge(chain, n * per + done[key])
                return link

            def ended(chain, per):
                assert done[chain.name] == per, (chain.name, done[chain.name], per)

            def combine(e, m, wide, first):
                dve.wait_ge(down, m * E + e + 1)
                if e:
                    dve.wait_ge(combined, m * E + e)
                nc.vector.tensor_tensor(y_b[:], down_bank(e, wide)[:, 0:T].rearrange("p (c d) -> p c d", c=TC),
                                        b_2[:, e:e + 1, :].to_broadcast([P, TC, D]), ALU.add).then_inc(biased, 1)
                dve.wait_ge(biased, m * E + e + 1)
                to = acc
                if e == E - 1:
                    to = acc_out
                    if not first:
                        dve.wait_ge(left, 16 * m)
                for c in range(TC):
                    last = nc.vector.scalar_tensor_tensor(to[:, c * D:(c + 1) * D], y_b[:, c, :], onehot[:, c, e:e + 1],
                                                          acc[:, c * D:(c + 1) * D], ALU.mult, ALU.add)
                last.then_inc(combined, 1)

            def moments(link, src, width, ready):
                for c in range(TC):
                    last = nc.vector.bn_stats(stats[:, c, :], src[:, c * width:(c + 1) * width])
                link(last)
                nc.vector.memset(spacer[:], 0.0)
                for c in range(TC):
                    last = nc.vector.bn_aggr(mv[:, c, :], stats[:, c, :])
                link(last)
                nc.vector.tensor_scalar(var_eps[:], mv[:, :, 1], LN_EPS, None, ALU.add).then_inc(ready, 1)

            def normalise(dst, src, width):
                for c in range(TC):
                    last = nc.vector.tensor_scalar(dst[:, c, 0:width], src[:, c * width:(c + 1) * width], mv[:, c, 0:1],
                                                   rstd[:, c:c + 1], ALU.subtract, ALU.mult)
                return last

            def normalise_full(b):
                dve.wait_ge(f_n.rstd, b + 1)
                for c in range(TC):
                    last = nc.vector.tensor_scalar(z_f[:, c, :].rearrange("p (r g) -> p g r", g=NP),
                                                   x_in[:, c * D:(c + 1) * D].rearrange("p (g r) -> p g r", g=NP),
                                                   mv[:, c, 0:1], rstd[:, c:c + 1], ALU.subtract, ALU.mult)
                last.then_inc(f_n.done, 1)

            def centre(link, b):
                dve.wait_ge(f_n.t, b + 1)
                link(nc.vector.reduce_sum(mean[:, 0:1], SIDE[:, 0:T], AX))
                link(nc.vector.tensor_scalar(mean[:, 1:2], mean[:, 0:1], 1.0 / T, None, ALU.mult))
                nc.vector.tensor_scalar(qk_f[:, 0, :], SIDE[:, 0:T], mean[:, 1:2], None, ALU.subtract).then_inc(centred, 1)
                dve.wait_ge(centred, b + 1)

            def split(core, buf, link, n, which, src):
                parts, count = buf[0], n * core.parts + which + 1
                high, mid, low = (parts[x][:, which, :] for x in "hml")
                nc.vector.tensor_copy(high, src[:, which, :]).then_inc(core.high, 1)
                dve.wait_ge(core.high, count)
                link(nc.vector.tensor_tensor(rest[:, which, :], src[:, which, :], high, ALU.subtract))
                nc.vector.tensor_copy(mid, rest[:, which, :]).then_inc(core.mid, 1)
                dve.wait_ge(core.mid, count)
                nc.vector.tensor_tensor(low, rest[:, which, :], mid, ALU.subtract).then_inc(core.low, 1)

            def mask(core, buf, n):
                _, _, k_raw, k_stack = buf
                dve.wait_ge(core.stacked_k, n * (16 * len(K_TERMS)) + 16 * len(K_TERMS))
                for a, b in ((0, NP // G), (NP // G, NP)):
                    for v in range(2):
                        last = nc.vector.tensor_scalar(k_stack[0:ROWS, a:b, v, :], k_raw[:, a:b, :],
                                                       const("headmask")[0:ROWS, v:v + 1], None, ALU.mult)
                    last.then_inc(core.masked, 1)

            def divide(core, att, n, g):
                dve.wait_ge(core.out_t, n * G + g + 1)
                o = TR[:, 0:T].rearrange("p (c v r) -> p c v r", c=TC, r=QUAD)
                nc.vector.reciprocal(rsum[:, g, :, :], o[:, :, :, HD]).then_inc(core.recip, 1)
                dve.wait_ge(core.recip, n * G + g + 1)
                nc.vector.tensor_tensor(att[:, :, g * V:(g + 1) * V, :], o[:, :, :, 0:HD],
                                        rsum[:, g, :, :].unsqueeze(3).to_broadcast([P, TC, V, HD]), ALU.mult).then_inc(core.normed, 1)

            def attend(core, att, n, slot):
                def row_max(g, u):
                    c, i0, pairs, keys = core.q_units[u]
                    idx = g * core.nq + u
                    dve.wait_ge(core.scores_q, n * (G * core.nq) + idx + 1)
                    nc.vector.reduce_max(maxima[:, 2 * g + i0:2 * g + i0 + pairs, c, :],
                                         SQ[idx % 2][:, 0:2 * pairs * keys].rearrange("p (i v k) -> p i v k", i=pairs, k=keys),
                                         AX).then_inc(core.maxed, 1)

                row_max(0, 0)
                row_max(0, 1)
                slot(0)
                for u in range(2, core.nq):
                    row_max(0, u)
                for g in range(G):
                    more = g + 1 < G
                    if more:
                        row_max(g + 1, 0)
                    slot(4 * g + 1)
                    if more:
                        row_max(g + 1, 1)
                    slot(4 * g + 2)
                    slot(4 * g + 3)
                    if more:
                        for u in range(2, core.nq):
                            row_max(g + 1, u)
                    if g:
                        divide(core, att, n, g - 1)
                    slot(4 * g + 4)
                slot(SLOTS - 1)

            def one(r):
                if r.like == 1:
                    dve.wait_ge(loaded, ALL_LOADED)
                    for i, name in enumerate(("qmask0", "qmask1", "kmask0", "kmask1")):
                        last = nc.vector.tensor_copy(masks_b[:, i, :], const(name))
                    last.then_inc(masks_ready, 1)

                pro = chain_of(c_n.chain, CHAIN_PRO, r.core)
                post = chain_of(post_chain, CHAIN_POST, r.post)
                norm = chain_of(norm_chain, CHAIN_NORM, r.s)
                band = chain_of(band_chain, CHAIN_BAND, r.first)
                if r.next_full:
                    nxt = chain_of(f_n.chain, CHAIN_NEXT_FULL, r.next)
                else:
                    nxt = chain_of(b_n.chain, CHAIN_NEXT_BAND, r.next)

                def step(name):
                    kind, k = expert_of(name)
                    if kind == "c":
                        combine(k, r.experts, r.wide, r.like == 3)
                    elif name == "lat":
                        done[c_n.chain.name] = 0
                        dve.wait_ge(lat_copied, r.core + 1)
                        moments(pro, lat_sb, LAT, lat_var)
                    elif name == "q":
                        dve.wait_ge(lat_rstd, r.core + 1)
                        normalise(lat_n, lat_sb, LAT).then_inc(lat_done, 1)
                        dve.wait_ge(q_ps, r.core + 1)
                        rope(0, "cos_q", "sin_q", q_read, r.core)
                    elif name == "split_q":
                        split(causal, c_buf, pro, r.core, 0, qk_c)
                    elif name == "k":
                        dve.wait_ge(k_ps, r.core + 1)
                        rope(1, "cos_k", "sin_k", k_read, r.core)
                    elif name == "split_k":
                        split(causal, c_buf, pro, r.core, 1, qk_c)
                        ended(c_n.chain, CHAIN_PRO)
                    elif name == "mask":
                        mask(causal, c_buf, r.core)
                    elif name == "out":
                        divide(causal, att_c, r.post, G - 1)
                    elif name == "f_out":
                        divide(full, att_f, r.first, G - 1)
                        dve.wait_ge(full.normed, r.first * G + G)
                        if r.has_core:
                            dve.wait_ge(xz_done, r.core + 1)
                        dve.wait_ge(res_done, r.s + 1)
                        nc.vector.tensor_tensor(x_mid[:], x_res[:], att_f[:].rearrange("p c h e -> p (c h e)"), ALU.add).then_inc(x_mid_a, 1)
                        dve.wait_ge(x_mid_a, r.first + 1)
                    elif name == "y":
                        done[post_chain.name] = 0
                        dve.wait_ge(y_ps, r.post + 1)
                        nc.vector.tensor_tensor(y1[:].rearrange("p c d -> p (c d)"), SIDE[:, 0:T], z_old[:], ALU.add).then_inc(y1_done, 1)
                        if r.has_experts:
                            dve.wait_ge(combined, (r.experts + 1) * E)
                        nc.vector.tensor_tensor(acc[:], SIDE[:, 0:T], xz_old[:], ALU.add).then_inc(acc_ready, 1)
                        dve.wait_ge(y1_done, r.post + 1)
                        post(nc.vector.tensor_tensor(sq[:], y1[:], y1[:], ALU.mult))
                        post(nc.vector.reduce_sum(sqr[:], sq[:], AX))
                        nc.vector.tensor_scalar(ms[:], sqr[:], 1.0 / D, RMS_EPS, ALU.mult, ALU.add).then_inc(y_ms, 1)
                    elif name == "xm":
                        dve.wait_ge(y_rrms, r.post + 1)
                        for c in range(TC):
                            last = nc.vector.tensor_scalar(xm[:, c, :], y1[:, c, :], rrms[:, c:c + 1], None, ALU.mult)
                        last.then_inc(xm_done, 1)
                    elif name == "route_a":
                        dve.wait_ge(logit_ps, r.post + 1)
                        post(nc.vector.tensor_tensor(logits[:], SIDE[:, 0:TC * E].rearrange("p (c e) -> p c e", e=E),
                                                     b_gate[:].unsqueeze(1).to_broadcast([P, TC, E]), ALU.add))
                        post(nc.vector.reduce_max(lmax[:], logits[:], AX))
                        post(nc.vector.tensor_tensor(ranked[:], logits[:], lmax[:].unsqueeze(2).to_broadcast([P, TC, E]), ALU.is_equal))
                    elif name == "route_b":
                        post(nc.vector.tensor_tensor(ranked[:], ranked[:], const("priority").unsqueeze(1).to_broadcast([P, TC, E]), ALU.mult))
                        post(nc.vector.reduce_max(rmax[:], ranked[:], AX))
                        nc.vector.tensor_tensor(onehot[:], ranked[:], rmax[:].unsqueeze(2).to_broadcast([P, TC, E]), ALU.is_equal).then_inc(routed, 1)
                        dve.wait_ge(routed, r.post + 1)
                        ended(post_chain, CHAIN_POST)
                    elif name == "norm_a":
                        done[norm_chain.name] = 0
                        moments(norm, x_mid, D, c_n.var)
                    elif name == "norm_b":
                        dve.wait_ge(c_n.rstd, r.s + 1)
                        norm(nc.vector.tensor_tensor(sqr[:], rstd[:], rstd[:], ALU.mult))
                        norm(nc.vector.tensor_tensor(sqr[:], sqr[:], mv[:, :, 1], ALU.mult))
                        nc.vector.tensor_scalar(ms[:], sqr[:], RMS_EPS, None, ALU.add).then_inc(c_ms, 1)
                        if r.has_core:
                            dve.wait_ge(saved, r.core + 1)
                        normalise(z, x_mid, D).then_inc(c_n.done, 1)
                        dve.wait_ge(c_n.done, r.s + 1)
                        ended(norm_chain, CHAIN_NORM)
                    elif name == "norm_c":
                        dve.wait_ge(c_rrms, r.s + 1)
                        for c in range(TC):
                            last = nc.vector.tensor_scalar(zr[:, c, :], z[:, c, :], rrms[:, c:c + 1], None, ALU.mult)
                        last.then_inc(zr_done, 1)
                    elif name == "f_norm_a":
                        if r.next_full:
                            dve.wait_ge(x_loaded, 16 * r.next + 16)
                            done[f_n.chain.name] = 0
                            moments(nxt, x_in, D, f_n.var)
                        else:
                            dve.wait_ge(x_moved, 16 * r.next + 16)
                            done[b_n.chain.name] = 0
                            moments(nxt, x_in, D, b_n.var)
                            ended(b_n.chain, CHAIN_NEXT_BAND)
                    elif name == "f_norm_b":
                        if r.next_full:
                            normalise_full(r.next)
                        else:
                            dve.wait_ge(b_n.rstd, r.next + 1)
                            normalise(z_f, x_in, D).then_inc(b_n.done, 1)
                    elif name == "f_centre":
                        centre(nxt, r.next)
                    elif name == "f_split":
                        split(full, f_buf, nxt, r.next, 0, qk_f)
                        ended(f_n.chain, CHAIN_NEXT_FULL)
                    elif name == "f_mask":
                        mask(full, f_buf, r.next)
                    elif name == "b_t":
                        done[band_chain.name] = 0
                        dve.wait_ge(b_n.done, r.first + 1)
                        dve.wait_ge(res_done, r.s + 1)
                        nc.vector.tensor_tensor(xz[:], x_res[:], z_f[:].rearrange("p c d -> p (c d)"), ALU.add)
                    elif name == "b_s":
                        dve.wait_ge(s_ps, r.first + 1)
                        band(nc.vector.tensor_tensor(s_band[:].rearrange("p c k -> p (c k)"), SK[0][:, 0:TC * T], const("band"), ALU.add))
                        band(nc.vector.reduce_max(bmax[:], s_band[:], AX))
                        nc.vector.tensor_scalar(nmax[:], bmax[:], -1.0, None, ALU.mult).then_inc(bmax_done, 1)
                    elif name == "b_ra":
                        dve.wait_ge(p_done, r.first + 1)
                        band(nc.vector.reciprocal(r_band[:], sum_band[:]))
                        dve.wait_ge(ra_ps, r.first + 1)
                        for c in range(TC):
                            last = nc.vector.tensor_scalar(ra[:, c, :], SQ[0][:, c * D:(c + 1) * D], r_band[:, c:c + 1], 0.0,
                                                           ALU.mult, ALU.max)
                        band(last)
                    elif name == "b_end":
                        if r.has_core:
                            dve.wait_ge(xz_done, r.core + 1)
                        nc.vector.tensor_tensor(x_mid[:], xz[:], ra[:].rearrange("p c d -> p (c d)"), ALU.add).then_inc(x_mid_b, 1)
                        dve.wait_ge(x_mid_b, r.first + 1)
                        ended(band_chain, CHAIN_BAND)

                def rope(which, cos, sin, read, n):
                    nc.vector.tensor_tensor(rope_a[:], SIDE[:, 0:T], const(cos), ALU.mult)
                    nc.vector.tensor_tensor(rope_b[:], SIDE[:, T:2 * T], const(sin), ALU.mult).then_inc(read, 1)
                    dve.wait_ge(read, n + 1)
                    pro(nc.vector.tensor_tensor(qk_c[:, which, :], rope_a[:], rope_b[:], ALU.add))

                first, second = r.steps("dve")

                def slots(part):
                    def slot(i):
                        for name in part[i]:
                            step(name)
                    return slot

                if r.has_first and r.first_full:
                    attend(full, att_f, r.first, slots(first))
                else:
                    for i in range(SLOTS):
                        slots(first)(i)
                if r.has_core:
                    attend(causal, att_c, r.core, slots(second))
                else:
                    for i in range(SLOTS):
                        slots(second)(i)

            nxt0 = chain_of(f_n.chain, CHAIN_NEXT_FULL, 0, begin=True)
            dve.wait_ge(x_loaded, 16)
            moments(nxt0, x_in, D, f_n.var)
            normalise_full(0)
            centre(nxt0, 0)
            split(full, f_buf, nxt0, 0, 0, qk_f)
            mask(full, f_buf, 0)
            rounds(dve, one)

        @block.tensor
        def _(pe):
            pe.wait_ge(consts_loaded, 16)
            pe.wait_ge(consts_ready, 2)

            def mm(o, lhs_t, rhs, start=True, stop=True):
                return nc.tensor.matmul(o, lhs_t, rhs, start=start, stop=stop)

            def up_product(k, m, wide, first=False, core_before=True):
                e, u = divmod(k, 2)
                ps = up_bank(k, wide)
                if k == 0:
                    pe.wait_ge(xm_tsb, m + 1)
                if not wide or k == 2:
                    if k == 0 and not first:
                        pe.wait_ge(biased, m * E)
                    elif k % 2 and k > 2:
                        pe.wait_ge(biased, m * E + k // 2)
                    elif k:
                        pe.wait_ge(relu, m * (2 * E) + k)
                elif k == 3:
                    if core_before:
                        pe.wait_ge(causal.normed, (m + 2) * G)
                else:
                    pe.wait_ge(relu, m * (2 * E) + k - 1)
                for i in range(2):
                    j = 2 * u + i
                    last = mm(ps[:, i * T:(i + 1) * T], w_1[:, e, j * P:(j + 1) * P], xm_t[:])
                last.then_inc(up, 1)

            def down_product(e, m, wide, core_before):
                ps = down_bank(e, wide)
                pe.wait_ge(relu, m * (2 * E) + min(2 * e + (2 if wide else 3), 2 * E))
                if wide and 0 < e < E - 1:
                    pe.wait_ge(biased, m * E + e)
                elif wide and e == 0 and core_before:
                    pe.wait_ge(causal.weighted_sb, (m + 2) * G)
                for c in range(TC):
                    for j in range(J):
                        last = mm(ps[:, c * D:(c + 1) * D], hidden[:, e % 2, j, c * P:(c + 1) * P], w_2[:, e, j, :],
                                  start=j == 0, stop=j == J - 1)
                last.then_inc(down, 1)

            def transpose2(dst, src, done):
                for c in range(TC):
                    last = nc.tensor.transpose(dst[:, c * P:(c + 1) * P], src(c), ident)
                last.then_inc(done, 1)

            def transpose_out(core, n, g):
                pe.wait_ge(core.weighted_sb, n * G + g + 1)
                pe.wait_ge(core.shift, n * G + min(g + 2, G))
                if g:
                    pe.wait_ge(core.normed, n * G + g)
                transpose2(TR, lambda c: wt_sb[:, g % 2, c * P:(c + 1) * P], core.out_t)

            def attend(core, buf, values, n, tr_free, wt_free, slot):
                _, q_stack, _, k_stack = buf

                def query_side(g, u):
                    c, i0, pairs, keys = core.q_units[u]
                    idx = g * core.nq + u
                    ps = SQ[idx % 2]
                    if idx >= 2:
                        pe.wait_ge(core.maxed, n * (G * core.nq) + idx - 1)
                    if core.causal:
                        mm(ps[:], ident_b[:], masks_b[:, QM0 if c == 0 else QM1, :], stop=False)
                    w = 2 * keys
                    for i in range(pairs):
                        pair = 2 * g + i0 + i
                        last = mm(ps[:, i * w:(i + 1) * w].rearrange("p (v k) -> p v k", k=keys),
                                  q_stack[0:ROWS, pair, c * P:(c + 1) * P], k_stack[0:ROWS, pair, :, 0:keys],
                                  start=not core.causal, stop=not core.causal or i == pairs - 1)
                    last.then_inc(core.scores_q, 1)

                def transpose_max(g):
                    pe.wait_ge(core.maxed, n * (G * core.nq) + (g + 1) * core.nq)
                    if g == 0 and tr_free:
                        pe.wait_ge(*tr_free)
                    if g >= 2:
                        pe.wait_ge(core.normed, n * G + g - 1)
                    for i in range(2):
                        for c in range(TC):
                            last = nc.tensor.transpose(tr_max[ROWS:ALL_ROWS, i * T + c * P:i * T + (c + 1) * P],
                                                       maxima[:, 2 * g + i, c, :], ident_b[:])
                    last.then_inc(core.max_t, 1)

                def key_side(g, u):
                    kc, i0, pairs, q0 = core.k_units[u]
                    idx = g * core.nk + u
                    ps = SK[idx % 2]
                    if u == 0:
                        pe.wait_ge(core.shift, n * G + g + 1)
                    if idx >= 2:
                        pe.wait_ge(core.probs, n * (G * core.nk) + idx - 1)
                    w = T - q0
                    if core.causal:
                        mm(ps[:], ident_b[:], masks_b[:, KM0 if kc == 0 else KM1, :], stop=False)
                    for i in range(2 * pairs):
                        pair, v = 2 * g + i0 + i // 2, i % 2
                        last = mm(ps[:, i * w:(i + 1) * w], k_stack[0:ALL_ROWS, pair, v, kc * P:(kc + 1) * P],
                                  q_stack[0:ALL_ROWS, pair, q0:T], start=not core.causal,
                                  stop=not core.causal or i == 2 * pairs - 1)
                    last.then_inc(core.scores_k, 1)

                def weigh(g):
                    pe.wait_ge(core.probs, n * (G * core.nk) + (g + 1) * core.nk)
                    if g:
                        pe.wait_ge(core.weighted_sb, n * G + g)
                    elif wt_free:
                        pe.wait_ge(*wt_free)
                    for kc in range(TC):
                        q0 = P if core.causal and kc else 0
                        for v in range(V):
                            last = mm(WT[v * QUAD:(v + 1) * QUAD, q0:T], values[:, kc, g * V + v, :],
                                      probs[:, g % 2, kc, v, q0:T], start=kc == 0, stop=kc == TC - 1)
                    last.then_inc(core.weighted, 1)

                pe.wait_ge(core.stacked_q, n * (16 * len(Q_TERMS)) + 16 * len(Q_TERMS))
                pe.wait_ge(core.masked, 2 * n + 1)
                query_side(0, 0)
                query_side(0, 1)
                slot(0)
                for u in range(2, core.nq):
                    query_side(0, u)
                pe.wait_ge(core.masked, 2 * n + 2)
                for g in range(G):
                    more = g + 1 < G
                    if more:
                        query_side(g + 1, 0)
                    slot(4 * g + 1)
                    if more:
                        query_side(g + 1, 1)
                    transpose_max(g)
                    if g == 1:
                        pe.wait_ge(core.values, n + 1)
                    if g:
                        weigh(g - 1)
                    slot(4 * g + 2)
                    key_side(g, 0)
                    key_side(g, 1)
                    slot(4 * g + 3)
                    if more:
                        for u in range(2, core.nq):
                            query_side(g + 1, u)
                    if g:
                        transpose_out(core, n, g - 1)
                    for u in range(2, core.nk):
                        key_side(g, u)
                    slot(4 * g + 4)
                weigh(G - 1)
                slot(SLOTS - 1)

            def transpose_full(b):
                pe.wait_ge(f_n.done, b + 1)
                transpose2(SIDE, lambda c: z_f[:, c, :], f_n.t)

            def one(r):
                n = r.core
                if r.like == 1:
                    pe.wait_ge(loaded, ALL_LOADED)
                    pe.wait_ge(masks_ready, 1)

                def step(name):
                    kind, k = expert_of(name)
                    if kind == "u":
                        up_product(k, r.experts, r.wide, core_before=r.has_post)
                    elif kind == "n":
                        up_product(k, r.post, False, not r.has_experts)
                    elif kind == "d":
                        down_product(k, r.experts, r.wide, r.has_post)
                    elif name == "zr_t":
                        pe.wait_ge(zr_done, n + 1)
                        if r.has_experts:
                            pe.wait_ge(routed, r.experts + 1)
                        transpose2(SIDE, lambda c: zr[:, c, :], c_n.t)
                    elif name == "lat":
                        pe.wait_ge(c_n.t_sb, n + 1)
                        for c in range(TC):
                            last = mm(SIDE[:, c * LAT:(c + 1) * LAT], z_t[:, c * P:(c + 1) * P], w_dkv[:])
                        last.then_inc(lat_ps, 1)
                    elif name == "q":
                        pe.wait_ge(lat_copied, n + 1)
                        mm(SIDE[:, 0:T], w_q[:], z_t[:])
                        mm(SIDE[:, T:2 * T], w_qr[:], z_t[:]).then_inc(q_ps, 1)
                    elif name == "lat_t":
                        pe.wait_ge(lat_done, n + 1)
                        pe.wait_ge(q_read, n + 1)
                        transpose2(SIDE, lambda c: lat_n[:, c, :], lat_tps)
                    elif name == "k":
                        pe.wait_ge(lat_tsb, n + 1)
                        mm(SIDE[:, 0:T], w_uk[:], lat_t[:])
                        mm(SIDE[:, T:2 * T], w_ukr[:], lat_t[:]).then_inc(k_ps, 1)
                    elif name == "v":
                        pe.wait_ge(k_read, n + 1)
                        for c in range(TC):
                            last = mm(SIDE[:, c * D:(c + 1) * D], lat_t[:, c * P:(c + 1) * P], w_uv[:])
                        last.then_inc(v_ps, 1)
                    elif name == "f_out":
                        transpose_out(full, r.first, G - 1)
                    elif name == "out":
                        transpose_out(causal, r.post, G - 1)
                    elif name == "att_t":
                        pe.wait_ge(causal.normed, r.post * G + G)
                        if r.has_next and r.next_full:
                            pe.wait_ge(centred, r.next + 1)
                        elif r.has_core:
                            pe.wait_ge(causal.values, n + 1)
                        transpose2(SIDE, lambda c: att_c[:, c, :, :].rearrange("p h e -> p (h e)"), att_tps)
                    elif name == "y":
                        pe.wait_ge(att_tsb, r.post + 1)
                        for c in range(TC):
                            last = mm(SIDE[:, c * D:(c + 1) * D], att_t[:, c * P:(c + 1) * P], w_o[:])
                        last.then_inc(y_ps, 1)
                    elif name == "xm_t":
                        pe.wait_ge(xm_done, r.post + 1)
                        transpose2(SIDE, lambda c: xm[:, c, :], xm_tps)
                    elif name == "logit":
                        pe.wait_ge(xm_tsb, r.post + 1)
                        for c in range(TC):
                            last = mm(SIDE[:, c * E:(c + 1) * E], xm_t[:, c * P:(c + 1) * P], w_gate[:])
                        last.then_inc(logit_ps, 1)
                    elif name == "f_t":
                        if r.has_core:
                            pe.wait_ge(causal.values, n + 1)
                        transpose_full(r.next)
                    elif name == "b_t":
                        pe.wait_ge(b_n.done, r.first + 1)
                        transpose2(SQ[0], lambda c: z_f[:, c, :], b_n.t)
                    elif name == "b_w":
                        pe.wait_ge(b_n.t_sb, r.first + 1)
                        mm(SQ[1][:, 0:T], w_b[:], z_bt[:]).then_inc(t_ps, 1)
                    elif name == "b_s":
                        pe.wait_ge(t_sb, r.first + 1)
                        for c in range(TC):
                            last = mm(SK[0][:, c * T:(c + 1) * T], t_t[:, c * P:(c + 1) * P], z_bt[:])
                        last.then_inc(s_ps, 1)
                    elif name == "b_pt":
                        pe.wait_ge(p_done, r.first + 1)
                        for kc in range(TC):
                            for c in range(TC):
                                last = nc.tensor.transpose(SK[1][:, kc * T + c * P:kc * T + (c + 1) * P],
                                                           p_band[:, c, kc * P:(kc + 1) * P], ident)
                        last.then_inc(pt_ps, 1)
                    elif name == "b_ra":
                        pe.wait_ge(pt_sb, r.first + 1)
                        for c in range(TC):
                            for kc in range(TC):
                                last = mm(SQ[0][:, c * D:(c + 1) * D], pt_band[:, kc, c * P:(c + 1) * P], z_f[:, kc, :],
                                          start=kc == 0, stop=kc == TC - 1)
                        last.then_inc(ra_ps, 1)

                first, second = r.steps("pe")

                def slots(part):
                    def slot(i):
                        for name in part[i]:
                            step(name)
                    return slot

                if r.has_first and r.first_full:
                    tr_free = (causal.normed, (r.s - 1) * G) if r.like >= 2 else None
                    attend(full, f_buf, values_f, r.first, tr_free, None, slots(first))
                else:
                    for i in range(SLOTS):
                        slots(first)(i)
                if r.has_core:
                    if r.has_first and r.first_full:
                        tr_free = (full.normed, (r.first + 1) * G)
                    else:
                        tr_free = None
                        if r.wide and r.has_experts:
                            tr_free = (relu, (r.experts + 1) * (2 * E))
                        elif r.like >= 2:
                            tr_free = (causal.normed, (r.s - 1) * G)
                    wt_free = (biased, (r.experts + 1) * E - 1) if r.wide and r.has_experts else None
                    attend(causal, c_buf, values_c, n, tr_free, wt_free, slots(second))
                else:
                    for i in range(SLOTS):
                        slots(second)(i)

            transpose_full(0)
            rounds(pe, one)


def constants():
    import numpy as np

    c = np.zeros((P, CST_COLS), np.float32)

    def put(name, a):
        c[:, CST[name][0]:CST[name][1]] = a

    r = np.arange(P)
    put("ident", np.eye(P, dtype=np.float32))
    later_key = np.where(r[None, :] > r[:, None], np.float32(-BIG), np.float32(0))
    zero = np.zeros((P, P), np.float32)
    put("qmask0", np.tile(later_key, (1, V)))
    put("qmask1", np.tile(np.concatenate([zero, later_key], 1), (1, 2)))
    put("kmask0", np.tile(np.concatenate([later_key.T, zero], 1), (1, 2)))
    put("kmask1", np.tile(later_key.T, (1, V)))
    k = np.arange(T)
    put("band", np.concatenate([np.where(np.abs(c0 * P + r[:, None] - k[None, :]) > BAND, np.float32(-BIG), np.float32(0))
                                for c0 in range(TC)], 1))
    half = HD // 2
    inv = (1.0 / np.float32(10000.0) ** (np.arange(half, dtype=np.float32) / np.float32(half))).astype(np.float32)
    ang = np.arange(T, dtype=np.float32)[:, None] * inv[None, :]
    dim = (r // NP) % HD
    cos, sin = np.cos(ang).T[dim % half], np.sin(ang).T[dim % half] * np.where(dim < half, -1, 1)[:, None]
    scale = 1.0 / np.sqrt(HD)
    put("cos_q", cos * scale)
    put("sin_q", sin * scale)
    put("cos_k", cos)
    put("sin_k", sin)
    put("headmask", (r % TERM)[:, None] // HD == np.arange(2)[None, :])
    put("shiftsel", -((r - ROWS)[:, None] == np.arange(2)[None, :]).astype(np.float32))
    put("priority", np.arange(E, 0, -1)[None, :])
    return c


def kernel(**inputs):
    import numpy as np
    import concourse.bacc as bacc
    from concourse.bass_utils import run_bass_kernel_spmd

    a = {k.replace("L0_", ""): np.asarray(v) for k, v in inputs.items()}
    order = np.arange(D).reshape(NP, TERM).T.reshape(-1)
    partner = (order // HD) * HD + (order % HD + HD // 2) % HD
    pad = np.zeros(D - LAT, np.float32)
    arrays = {
        "x": a["attn_a_x"], "wb": a["attn_b_W"],
        "wq": a["ffn_Wq"].T[:, order], "wqr": a["ffn_Wq"].T[:, partner],
        "wdkv": a["ffn_Wdkv"].T,
        "wuk": a["ffn_Wuk"].T[:, order], "wukr": a["ffn_Wuk"].T[:, partner], "wuv": a["ffn_Wuv"].T,
        "wo": a["ffn_Wo"].T, "gate": a["ffn_gate_w"].T,
        "w1": a["ffn_W1"].transpose(2, 0, 1),
        "w2": a["ffn_W2"].reshape(E, D, J, P).transpose(3, 0, 2, 1),
        "b1": a["ffn_b1"].reshape(E * J, P).T,
        "b2": np.broadcast_to(a["ffn_b2"][None], (P, E, D)),
        "gate_b": np.broadcast_to(a["ffn_gate_b"][None], (P, E)),
        "cols": np.stack([a["ffn_norm1_w"], a["ffn_norm2_w"], np.concatenate([a["ffn_ln_g"], pad]),
                          np.concatenate([a["ffn_ln_b"], pad])], 1),
        "cst": constants(),
    }
    arrays = {k: np.ascontiguousarray(v) for k, v in arrays.items()}
    nc = bacc.Bacc("TRN2", target_bir_lowering=False, num_devices=1)
    args = [nc.dram_tensor(f"in_{k}", v.shape, mybir.dt.from_np(v.dtype), kind="ExternalInput").ap()
            for k, v in arrays.items()]
    out = nc.dram_tensor("out_x", (B, T, D), F32, kind="ExternalOutput").ap()
    build(nc, *args, out)
    r = run_bass_kernel_spmd(nc, [{f"in_{k}": v for k, v in arrays.items()}], core_ids=[0])
    return r.results[0]["out_x"]
```
